# Optimizing a Trainium2 kernel written in Bass

```python
import numpy as np
import jax
import jax.numpy as jnp

def _softmax(x, axis=-1):
    return jax.nn.softmax(x, axis=axis)

def _gelu(x):
    return jax.nn.gelu(x, approximate=True)

def _silu(x):
    return jax.nn.silu(x)

def _sigmoid(x):
    return jax.nn.sigmoid(x)

def _layernorm(x, axis=-1, eps=1e-05):
    m = jnp.mean(x, axis=axis, keepdims=True)
    v = jnp.var(x, axis=axis, keepdims=True)
    return (x - m) / jnp.sqrt(v + eps)

def _scatter_add(tgt, idx, src, axis=0):
    return tgt.at[idx].add(src)

def _segment_sum(src, seg, n):
    return jax.ops.segment_sum(src, seg, n)
kernel_name = 'mk_xattn_ffn_d1_seqx_r4_78718a'

def setup_inputs(seed: int=0):
    np.random.seed(seed)
    _w = jnp.asarray

    def _rec_inputs():
        import jax
        import jax.numpy as jnp
        _rk = jax.random.key(seed)
        x = 0.01048 + 0.1018 * jax.random.normal(jax.random.fold_in(_rk, 1), (4, 512, 512), jnp.float32)
        _lenS = 512 - jax.random.randint(jax.random.fold_in(_rk, 7), (4,), 0, max(1, 512 // 4) + 1, jnp.int32)
        _lenS2 = 512 - jax.random.randint(jax.random.fold_in(_rk, 8), (4,), 0, max(1, 512 // 4) + 1, jnp.int32)
        _ctx_512P = jax.random.normal(jax.random.fold_in(_rk, 11), (4, 16, 128), jnp.float32)
        _ctx_512c = jax.random.dirichlet(jax.random.fold_in(_rk, 511), 0.3 * jnp.ones((16,), jnp.float32), (4, 512))
        _ctx_512t = jnp.einsum('bsk,bkd->bsd', _ctx_512c, _ctx_512P)
        _ctx_512t = _ctx_512t * jax.lax.rsqrt(jnp.mean(jnp.square(_ctx_512t)) + 1e-12) * 0.953939
        ctx_512 = -0.000292821 + 1.00034 * (_ctx_512t + 0.3 * jax.random.normal(jax.random.fold_in(_rk, 611), (4, 512, 128), jnp.float32))
        return (x, ctx_512)
    x, ctx_512 = _rec_inputs()

    def _L0_xattn_setup():
        import jax, jax.numpy as jnp
        import numpy as np
        LRELU_ALPHA = 0.2
        MASK_VAL = -10000000000.0
        B, N, F_IN = (4, 512, 128)
        H, F_OUT = (8, 64)
        F_HID = H * F_OUT

        def gat_layer(x, adj, W, a_self, a_neigh, b):
            feat = jnp.einsum('nf,hfo->hno', x, W)
            attn_self = jnp.einsum('hno,ho->hn', feat, a_self)
            attn_neigh = jnp.einsum('hno,ho->hn', feat, a_neigh)
            e = attn_self[:, :, None] + attn_neigh[:, None, :]
            e = jax.nn.leaky_relu(e, LRELU_ALPHA)
            e = e + MASK_VAL * (1.0 - adj)[None, :, :]
            alpha = jax.nn.softmax(e, axis=-1)
            out = jnp.einsum('hnm,hmo->hno', alpha, feat) + b[:, None, :]
            out = jnp.transpose(out, (1, 0, 2)).reshape(out.shape[1], -1)
            return jax.nn.elu(out)
        key = jax.random.key(seed)
        ks = jax.random.split(key, 10)
        feats = jax.random.normal(ks[0], (B, N, F_IN), dtype=jnp.float32)
        a = (jax.random.uniform(ks[1], (B, N, N)) < 0.01).astype(jnp.float32)
        adj = jnp.maximum(a, jnp.eye(N, dtype=jnp.float32)[None])
        s0 = 1.0 / np.sqrt(F_IN)
        s1 = 1.0 / np.sqrt(F_HID)
        return {'feats': feats, 'adj': adj, 'W0': jax.random.normal(ks[2], (H, F_IN, F_OUT), dtype=jnp.float32) * s0, 'a_self0': jax.random.normal(ks[3], (H, F_OUT), dtype=jnp.float32) * 0.1, 'a_neigh0': jax.random.normal(ks[4], (H, F_OUT), dtype=jnp.float32) * 0.1, 'b0': jnp.zeros((H, F_OUT), dtype=jnp.float32), 'W1': jax.random.normal(ks[5], (H, F_HID, F_OUT), dtype=jnp.float32) * s1, 'a_self1': jax.random.normal(ks[6], (H, F_OUT), dtype=jnp.float32) * 0.1, 'a_neigh1': jax.random.normal(ks[7], (H, F_OUT), dtype=jnp.float32) * 0.1, 'b1': jnp.zeros((H, F_OUT), dtype=jnp.float32)}
    _L0_xattn_all = _L0_xattn_setup()
    _L0_xattn_in = {k: v for k, v in _L0_xattn_all.items() if k in ('W0', 'a_self0', 'a_neigh0', 'b0', 'W1', 'a_self1', 'a_neigh1', 'b1')}
    del _L0_xattn_all

    def _L0_ffn_setup():
        import jax, jax.numpy as jnp
        import numpy as np
        E = 64
        K = 6
        CAP = 128
        SCALE = 1.0
        H = 512
        I = 192
        SI = I * 2
        B, S = (2, 256)

        def _moe(x, gate_w, gate_up_proj, down_proj, shared_gate_w, shared_up_w, shared_down_w):
            b, s, h = x.shape
            T = b * s
            xf = x.reshape(T, h)
            scores = jax.nn.softmax(xf @ gate_w.T, axis=-1)
            topk_w, topk_idx = jax.lax.top_k(scores, K)
            topk_w = topk_w * SCALE
            flat_e = topk_idx.reshape(-1)
            order = jnp.argsort(flat_e)
            sorted_e = flat_e[order]
            sorted_tok = (order // K).astype(jnp.int32)
            sorted_w = topk_w.reshape(-1)[order]
            counts = jnp.zeros((E,), jnp.int32).at[flat_e].add(1)
            offsets = jnp.cumsum(counts) - counts
            pos = jnp.arange(T * K, dtype=jnp.int32) - offsets[sorted_e]
            buf_tok = jnp.full((E, CAP), T, jnp.int32).at[sorted_e, pos].set(sorted_tok, mode='drop')
            buf_w = jnp.zeros((E, CAP), x.dtype).at[sorted_e, pos].set(sorted_w, mode='drop')
            xp = jnp.concatenate([xf, jnp.zeros((1, h), x.dtype)], axis=0)
            gx = xp[buf_tok]
            gu = jnp.einsum('ech,ehi->eci', gx, gate_up_proj)
            g, u = jnp.split(gu, 2, axis=-1)
            hid = jax.nn.silu(g) * u
            eo = jnp.einsum('eci,eih->ech', hid, down_proj) * buf_w[..., None]
            routed = jnp.zeros((T + 1, h), x.dtype).at[buf_tok.reshape(-1)].add(eo.reshape(-1, h))[:T]
            shared = jax.nn.silu(xf @ shared_gate_w.T) * (xf @ shared_up_w.T) @ shared_down_w.T
            return (routed + shared).reshape(b, s, h)
        key = jax.random.key(seed)
        ks = jax.random.split(key, 7)
        x = jax.random.normal(ks[0], (B, S, H), jnp.float32)
        gate_w = jax.random.normal(ks[1], (E, H), jnp.float32) * 0.02
        gate_up_proj = jax.random.normal(ks[2], (E, H, 2 * I), jnp.float32) * 0.02
        down_proj = jax.random.normal(ks[3], (E, I, H), jnp.float32) * 0.02
        shared_gate_w = jax.random.normal(ks[4], (SI, H), jnp.float32) * 0.02
        shared_up_w = jax.random.normal(ks[5], (SI, H), jnp.float32) * 0.02
        shared_down_w = jax.random.normal(ks[6], (H, SI), jnp.float32) * 0.02
        return dict(x=x, gate_w=gate_w, gate_up_proj=gate_up_proj, down_proj=down_proj, shared_gate_w=shared_gate_w, shared_up_w=shared_up_w, shared_down_w=shared_down_w)
    _L0_ffn_all = _L0_ffn_setup()
    _L0_ffn_in = {k: v for k, v in _L0_ffn_all.items() if k in ('gate_w', 'gate_up_proj', 'down_proj', 'shared_gate_w', 'shared_up_w', 'shared_down_w')}
    del _L0_ffn_all
    return {'x': x, 'ctx_512': ctx_512, 'L0_xattn_W0': _L0_xattn_in['W0'], 'L0_xattn_a_self0': _L0_xattn_in['a_self0'], 'L0_xattn_a_neigh0': _L0_xattn_in['a_neigh0'], 'L0_xattn_b0': _L0_xattn_in['b0'], 'L0_xattn_W1': _L0_xattn_in['W1'], 'L0_xattn_a_self1': _L0_xattn_in['a_self1'], 'L0_xattn_a_neigh1': _L0_xattn_in['a_neigh1'], 'L0_xattn_b1': _L0_xattn_in['b1'], 'L0_ffn_gate_w': _L0_ffn_in['gate_w'], 'L0_ffn_gate_up_proj': _L0_ffn_in['gate_up_proj'], 'L0_ffn_down_proj': _L0_ffn_in['down_proj'], 'L0_ffn_shared_gate_w': _L0_ffn_in['shared_gate_w'], 'L0_ffn_shared_up_w': _L0_ffn_in['shared_up_w'], 'L0_ffn_shared_down_w': _L0_ffn_in['shared_down_w']}

def reference(x, ctx_512, L0_xattn_W0, L0_xattn_a_self0, L0_xattn_a_neigh0, L0_xattn_b0, L0_xattn_W1, L0_xattn_a_self1, L0_xattn_a_neigh1, L0_xattn_b1, L0_ffn_gate_w, L0_ffn_gate_up_proj, L0_ffn_down_proj, L0_ffn_shared_gate_w, L0_ffn_shared_up_w, L0_ffn_shared_down_w):
    import jax
    import jax.numpy as jnp

    def _L0_xattn_ref(feats, adj, W0, a_self0, a_neigh0, b0, W1, a_self1, a_neigh1, b1):
        import jax, jax.numpy as jnp
        import numpy as np
        LRELU_ALPHA = 0.2
        MASK_VAL = -10000000000.0
        B, N, F_IN = (4, 512, 128)
        H, F_OUT = (8, 64)
        F_HID = H * F_OUT

        def gat_layer(x, adj, W, a_self, a_neigh, b):
            feat = jnp.einsum('nf,hfo->hno', x, W)
            attn_self = jnp.einsum('hno,ho->hn', feat, a_self)
            attn_neigh = jnp.einsum('hno,ho->hn', feat, a_neigh)
            e = attn_self[:, :, None] + attn_neigh[:, None, :]
            e = jax.nn.leaky_relu(e, LRELU_ALPHA)
            e = e + MASK_VAL * (1.0 - adj)[None, :, :]
            alpha = jax.nn.softmax(e, axis=-1)
            out = jnp.einsum('hnm,hmo->hno', alpha, feat) + b[:, None, :]
            out = jnp.transpose(out, (1, 0, 2)).reshape(out.shape[1], -1)
            return jax.nn.elu(out)

        def per_graph(x, a):
            h = gat_layer(x, a, W0, a_self0, a_neigh0, b0)
            return gat_layer(h, a, W1, a_self1, a_neigh1, b1)
        return jax.vmap(per_graph)(feats, adj)

    def _L0_ffn_ref(x, gate_w, gate_up_proj, down_proj, shared_gate_w, shared_up_w, shared_down_w):
        import jax, jax.numpy as jnp
        import numpy as np
        E = 64
        K = 6
        CAP = 128
        SCALE = 1.0
        H = 512
        I = 192
        SI = I * 2
        B, S = (2, 256)

        def _moe(x, gate_w, gate_up_proj, down_proj, shared_gate_w, shared_up_w, shared_down_w):
            b, s, h = x.shape
            T = b * s
            xf = x.reshape(T, h)
            scores = jax.nn.softmax(xf @ gate_w.T, axis=-1)
            topk_w, topk_idx = jax.lax.top_k(scores, K)
            topk_w = topk_w * SCALE
            flat_e = topk_idx.reshape(-1)
            order = jnp.argsort(flat_e)
            sorted_e = flat_e[order]
            sorted_tok = (order // K).astype(jnp.int32)
            sorted_w = topk_w.reshape(-1)[order]
            counts = jnp.zeros((E,), jnp.int32).at[flat_e].add(1)
            offsets = jnp.cumsum(counts) - counts
            pos = jnp.arange(T * K, dtype=jnp.int32) - offsets[sorted_e]
            buf_tok = jnp.full((E, CAP), T, jnp.int32).at[sorted_e, pos].set(sorted_tok, mode='drop')
            buf_w = jnp.zeros((E, CAP), x.dtype).at[sorted_e, pos].set(sorted_w, mode='drop')
            xp = jnp.concatenate([xf, jnp.zeros((1, h), x.dtype)], axis=0)
            gx = xp[buf_tok]
            gu = jnp.einsum('ech,ehi->eci', gx, gate_up_proj)
            g, u = jnp.split(gu, 2, axis=-1)
            hid = jax.nn.silu(g) * u
            eo = jnp.einsum('eci,eih->ech', hid, down_proj) * buf_w[..., None]
            routed = jnp.zeros((T + 1, h), x.dtype).at[buf_tok.reshape(-1)].add(eo.reshape(-1, h))[:T]
            shared = jax.nn.silu(xf @ shared_gate_w.T) * (xf @ shared_up_w.T) @ shared_down_w.T
            return (routed + shared).reshape(b, s, h)
        return _moe(x, gate_w, gate_up_proj, down_proj, shared_gate_w, shared_up_w, shared_down_w)
    x = x + _L0_xattn_ref(ctx_512, _layernorm(x, axis=-1), L0_xattn_W0, L0_xattn_a_self0, L0_xattn_a_neigh0, L0_xattn_b0, L0_xattn_W1, L0_xattn_a_self1, L0_xattn_a_neigh1, L0_xattn_b1)
    x = x + _L0_ffn_ref(_layernorm(x, axis=-1), L0_ffn_gate_w, L0_ffn_gate_up_proj, L0_ffn_down_proj, L0_ffn_shared_gate_w, L0_ffn_shared_up_w, L0_ffn_shared_down_w)
    return x

_drawn_inputs = setup_inputs


def setup_inputs(seed=0):
    import zlib

    import numpy as np

    out = dict(_drawn_inputs(seed))
    spreads = {'L0_xattn_b0': (0.0, 0.1), 'L0_xattn_b1': (0.0, 0.1)}
    factors = {'L0_ffn_gate_w': 8.0,
     'L0_ffn_gate_up_proj': 8.0,
     'L0_ffn_down_proj': 8.0,
     'L0_ffn_shared_gate_w': 8.0,
     'L0_ffn_shared_up_w': 8.0,
     'L0_ffn_shared_down_w': 8.0}
    for name, (base, spread) in spreads.items():
        noise = np.random.default_rng([zlib.crc32(name.encode()), seed]).standard_normal(out[name].shape)
        drawn = base * np.exp(spread * noise) if base else spread * noise
        out[name] = jnp.asarray(drawn.astype(out[name].dtype))
    for name, factor in factors.items():
        out[name] = (out[name] * factor).astype(out[name].dtype)
    return out
```

```python
from contextlib import ExitStack

import concourse.bass as bass
import concourse.mybir as mybir

F32 = mybir.dt.float32
U32 = mybir.dt.uint32
I32 = mybir.dt.int32
ALU = mybir.AluOpType
ACT = mybir.ActivationFunctionType
AX_X = mybir.AxisListType.X
RMAX = bass.bass_isa.ReduceOp.max

P = 128
B, N, D = 4, 512, 512
FIN, H, O = 128, 8, 64
T = B * N
NT = T // P
TB = N // P
KC = D // P
E, TOPK, CAP = 64, 6, 128
I = 192
IH = I // 2
SI = 2 * I
SC = SI // P
ROW = D + E
EPS = 1e-5
LRELU = 0.2
MASK_VAL = -1e10
U = 4
EXP_FLOOR = -87.336
HALF = T // 2
FORCE_GENERAL = False


def due(value):
    return not (isinstance(value, int) and value <= 0)


def turns(engine, n):
    yield 0
    with engine.Fori(1, n) as i:
        yield i




class Kernel:
    pass


def allocate(nc, ctx, k):
    def sb(name, shape, dt=F32):
        return ctx.enter_context(nc.sbuf_tensor(name, shape, dt))

    k.x = sb("x", [P, NT, D])
    k.ident = sb("ident", [P, P])
    k.ones = sb("ones", [P, P])
    k.flag = sb("flag", [1, 1], I32)
    k.psum = [ctx.enter_context(nc.psum_tensor(f"bank{i}", [P, 512], F32)) for i in range(8)]


def attention_block(nc, k, a):
    with ExitStack() as ctx:
        def sb(name, shape, dt=F32):
            return ctx.enter_context(nc.sbuf_tensor(name, shape, dt))

        def sem(name):
            return ctx.enter_context(nc.semaphore(name))

        w0 = sb("w0", [P, H * O])
        w1 = sb("w1", [P, KC, H * O])
        absw = sb("absw", [P, KC + 1, H * O])
        b0t = sb("b0t", [P, KC])
        b1bc = sb("b1bc", [P, H * O])
        ctx_all = sb("ctx_all", [P, NT * FIN])
        small = sb("small", [H, 5, O])
        bounds = sb("bounds", [H, 8])
        bounds_max = sb("bounds_max", [H, 4])
        rowstat = sb("rowstat", [P, 2])
        rowstat_max = sb("rowstat_max", [P, 2])
        colsum = sb("colsum", [P, 2])
        fin = sb("fin", [1, 8])
        top = sb("top", [P, NT, 8])
        top_ix = sb("top_ix", [P, NT, 8], U32)
        node = sb("node", [P, NT], U32)
        node2 = sb("node2", [P, NT], U32)
        bn = sb("bn", [P, NT, 6])
        mv = sb("mv", [P, NT, 2])
        rstd = sb("rstd", [P, NT])
        gap = sb("gap", [P, NT])
        lead = sb("lead", [P, NT])
        mhalf = sb("mhalf", [P, NT])
        gath = sb("gath", [P, TB, FIN])
        gathT = sb("gathT", [P, N])
        h1T = sb("h1T", [P, KC, N])
        ex1 = sb("ex1", [P, 2, N])
        em1 = sb("em1", [P, 2, N])
        s2 = sb("s2", [P, 2, H * O])
        ex2 = sb("ex2", [P, 2, H * O])
        em2 = sb("em2", [P, 2, H * O])
        z2 = sb("z2", [P, 2, H * O])

        x_in = [sem(f"x_in{b}") for b in range(B)]
        w_in, small_in, w1_in, ctx_in = sem("w_in"), sem("small_in"), sem("w1_in"), sem("ctx_in")
        consts = sem("consts")
        vch = sem("vch")
        node_ready, node_stored, node2_in, gath_in = (sem(s) for s in ("node_ready", "node_stored", "node2_in", "gath_in"))
        gT_done, gT_sb = sem("gT_done"), sem("gT_sb")
        l1_done, l1_exp, l1_em, h1_ready = (sem(s) for s in ("l1_done", "l1_exp", "l1_em", "h1_ready"))
        l2_done, s2_ready, l2_exp, em2_ready, z2_ready, x2_ready = (sem(s) for s in ("l2_done", "s2_ready", "l2_exp", "em2_ready", "z2_ready", "x2_ready"))
        absw_done, colsum_done, abs_small, bounds_ready, reduced, rstd_ready, var_ready, rows_ready = (
            sem(s) for s in ("absw_done", "colsum_done", "abs_small", "bounds_ready", "reduced", "rstd_ready", "var_ready", "rows_ready"))
        pch = sem("pch")

        bank = k.psum
        GT, L1, L2 = bank[0], bank[1:3], bank[3:5]
        CS = bank[5:7]

        with nc.Block() as block:
            @block.sync
            def _(sp):
                for b in range(B):
                    sp.dma_start(k.x[:, b * TB:(b + 1) * TB, :],
                                 a["x"][b].rearrange("(t p) d -> p t d", p=P)).then_inc(x_in[b], 16)
                sp.dma_start(w0[:].rearrange("f (h o) -> f h o", h=H),
                             a["W0"].rearrange("h f o -> f h o")).then_inc(w_in, 16)
                sp.dma_start(b0t[:], a["b0"].rearrange("h o -> (h o)").rearrange("(c p) -> p c", p=P),
                             allow_slow_non_contiguous=True).then_inc(w_in, 16)
                sp.dma_start(b1bc[:], a["b1"].rearrange("h o -> (h o)").rearrange("(u d) -> u d", u=1)
                             .broadcast_to([P, H * O])).then_inc(w_in, 16)
                for c in range(KC):
                    sp.dma_start(w1[:, c, :].rearrange("f (h o) -> f h o", h=H),
                                 a["W1"][:, c * P:(c + 1) * P, :].rearrange("h f o -> f h o")).then_inc(w1_in, 16)
                for j, name in enumerate(("a_self0", "a_neigh0", "a_self1", "a_neigh1", "b0")):
                    sp.dma_start(small[:, j, :], a[name]).then_inc(small_in, 16)
                sp.dma_start(ctx_all[:].rearrange("p (r f) -> p r f", f=FIN),
                             a["ctx"].rearrange("(p r) f -> p r f", p=P)).then_inc(ctx_in, 16)

            @block.gpsimd
            def _(pool):
                nc.gpsimd.memset(k.ident[:], 0.0).then_inc(pch, 1)
                pool.wait_ge(pch, 1)
                nc.gpsimd.affine_select(out=k.ident[:], in_=k.ident[:], compare_op=ALU.not_equal, fill=1.0,
                                        base=0, pattern=[[-1, P]], channel_multiplier=1)
                nc.gpsimd.memset(k.ones[:], 1.0)
                nc.gpsimd.memset(mhalf[:], -0.5).then_inc(consts, 1)
                def gather(b):
                    pool.wait_ge(node_ready, b + 1)
                    pool.dma_start(a["node_dram"][b * N:(b + 1) * N, :].rearrange("(t p) u -> p (t u)", p=P),
                                   node[:, b * TB:(b + 1) * TB], allow_slow_non_contiguous=True).then_inc(node_stored, 16)
                    pool.wait_ge(node_stored, 16 * (b + 1))
                    for t in range(b * TB, (b + 1) * TB):
                        pool.indirect_dma_start(
                            node2[:, t:t + 1], None, a["node_dram"][:, :],
                            bass.IndirectOffsetOnAxis(ap=node[:, t:t + 1], axis=0)).then_inc(node2_in, 16)
                    pool.wait_ge(node2_in, 16 * TB * (b + 1))
                    if b:
                        if due(b):
                            pool.wait_ge(gT_done, b)
                    for t in range(TB):
                        pool.indirect_dma_start(
                            gath[:, t, :], None, a["ctx"][:, :],
                            bass.IndirectOffsetOnAxis(ap=node2[:, b * TB + t:b * TB + t + 1], axis=0)).then_inc(gath_in, 16)

                def add(b):
                    for t in range(b * TB, (b + 1) * TB):
                        pool.wait_ge(z2_ready, t + 1)
                        nc.gpsimd.tensor_tensor(k.x[:, t, :], k.x[:, t, :], z2[:, t % 2, :], ALU.add).then_inc(x2_ready, 1)

                gather(0)
                for b in range(B):
                    if b + 1 < B:
                        gather(b + 1)
                    add(b)
                pool.wait_ge(var_ready, 1)
                nc.gpsimd.tensor_tensor(rstd[:], rstd[:], mhalf[:], ALU.pow).then_inc(rstd_ready, 1)
                pool.wait_ge(bounds_ready, 1)
                nc.gpsimd.partition_all_reduce(bounds_max[:, 0:3], bounds[:, 0:3], H, RMAX).then_inc(reduced, 1)
                pool.wait_ge(rows_ready, 1)
                nc.gpsimd.partition_all_reduce(rowstat_max[:], rowstat[:], P, RMAX).then_inc(reduced, 1)

            @block.tensor
            def _(pe):
                pe.wait_ge(consts, 1)
                pe.wait_ge(absw_done, KC + 1)
                nc.tensor.matmul(CS[0][:], k.ones[:], absw[:, KC, :], start=True, stop=True)
                for c in range(KC):
                    last = nc.tensor.matmul(CS[1][:], k.ones[:], absw[:, c, :], start=(c == 0), stop=(c == KC - 1))
                last.then_inc(colsum_done, 1)
                pe.wait_ge(w_in, 48)
                pe.wait_ge(w1_in, 16 * KC)
                for b in turns(pe, B):
                    pe.wait_ge(gath_in, (b + 1) * (16 * TB))
                    for t in range(TB):
                        last = nc.tensor.transpose(GT[:, t * P:(t + 1) * P], gath[:, t, :], k.ident[:])
                    last.then_inc(gT_done, 1)
                    pe.wait_ge(gT_sb, b + 1)
                    for c in range(KC):
                        if c >= 2:
                            if due(b * KC + c - 1):
                                pe.wait_ge(h1_ready, b * KC + c - 1)
                        nc.tensor.matmul(L1[c % 2][:], w0[:, c * P:(c + 1) * P], gathT[:],
                                         start=True, stop=True).then_inc(l1_done, 1)
                    for t in range(TB):
                        if due(b * TB):
                            pe.wait_ge(s2_ready, b * TB)
                        if t >= 2:
                            if due(b * TB + t - 1):
                                pe.wait_ge(s2_ready, b * TB + t - 1)
                        for c in range(KC):
                            if t == 0:
                                pe.wait_ge(h1_ready, b * KC + c + 1)
                            last = nc.tensor.matmul(L2[t % 2][:], h1T[:, c, t * P:(t + 1) * P], w1[:, c, :],
                                                    start=(c == 0), stop=(c == KC - 1))
                        last.then_inc(l2_done, 1)

            @block.scalar
            def _(act):
                act.wait_ge(w_in, 48)
                nc.scalar.activation(absw[:, KC, :], w0[:], ACT.Abs).then_inc(absw_done, 1)
                act.wait_ge(w1_in, 16 * KC)
                for c in range(KC):
                    nc.scalar.activation(absw[:, c, :], w1[:, c, :], ACT.Abs).then_inc(absw_done, 1)
                act.wait_ge(small_in, 80)
                for j in range(4):
                    nc.scalar.activation(small[:, j, :], small[:, j, :], ACT.Abs,
                                         accum_out=bounds[:, 3 + j:4 + j]).then_inc(abs_small, 1)
                nc.scalar.activation(small[:, 4, :], small[:, 4, :], ACT.Abs).then_inc(abs_small, 1)
                act.wait_ge(ctx_in, 16)
                nc.scalar.activation(ctx_all[:], ctx_all[:], ACT.Abs).then_inc(abs_small, 1)
                for b in turns(act, B):
                    act.wait_ge(gT_done, b + 1)
                    if due(b * KC):
                        act.wait_ge(l1_done, b * KC)
                    nc.scalar.activation(gathT[:], GT[:], ACT.Copy).then_inc(gT_sb, 1)
                    for c in range(KC):
                        act.wait_ge(l1_done, b * KC + c + 1)
                        if due(b * KC + max(c - 1, 0)):
                            act.wait_ge(l1_em, b * KC + max(c - 1, 0))
                        nc.scalar.activation(ex1[:, c % 2, :], L1[c % 2][:], ACT.Exp,
                                             bias=b0t[:, c:c + 1]).then_inc(l1_exp, 1)
                    for t in range(TB):
                        act.wait_ge(s2_ready, b * TB + t + 1)
                        if due(b * TB + max(t - 1, 0)):
                            act.wait_ge(em2_ready, b * TB + max(t - 1, 0))
                        nc.scalar.activation(ex2[:, t % 2, :], s2[:, t % 2, :], ACT.Exp).then_inc(l2_exp, 1)

            @block.vector
            def _(dve):
                chain = [0]

                def link(ins):
                    chain[0] += 1
                    ins.then_inc(vch, 1)
                    dve.wait_ge(vch, chain[0])

                for b in range(B):
                    dve.wait_ge(x_in[b], 16)
                    for t in range(b * TB, (b + 1) * TB):
                        link(nc.vector.max(top[:, t, :], k.x[:, t, :]))
                        last = nc.vector.max_index(top_ix[:, t, :], top[:, t, :], k.x[:, t, :])
                    link(last)
                    nc.vector.tensor_scalar(node[:, b * TB:(b + 1) * TB], top_ix[:, b * TB:(b + 1) * TB, 0],
                                            float(b * N), None, ALU.add).then_inc(node_ready, 1)
                for t in range(NT):
                    last = nc.vector.bn_stats(bn[:, t, :], k.x[:, t, :])
                link(last)
                for t in range(NT):
                    last = nc.vector.bn_aggr(mv[:, t, :], bn[:, t, :])
                link(last)
                for b in turns(dve, B):
                    for c in range(KC):
                        dve.wait_ge(l1_exp, b * KC + c + 1)
                        if due(b * KC + max(c - 1, 0)):
                            dve.wait_ge(h1_ready, b * KC + max(c - 1, 0))
                        nc.vector.tensor_scalar(em1[:, c % 2, :], ex1[:, c % 2, :], 1.0, -1.0,
                                                ALU.min, ALU.add).then_inc(l1_em, 1)
                        dve.wait_ge(l1_em, b * KC + c + 1)
                        if c == 0:
                            if due(b * TB):
                                dve.wait_ge(l2_done, b * TB)
                        nc.vector.scalar_tensor_tensor(h1T[:, c, :], L1[c % 2][:], b0t[:, c:c + 1], em1[:, c % 2, :],
                                                       ALU.add, ALU.max).then_inc(h1_ready, 1)
                    def finish(t):
                        dve.wait_ge(l2_exp, b * TB + t + 1)
                        if due(b * TB + max(t - 1, 0)):
                            dve.wait_ge(z2_ready, b * TB + max(t - 1, 0))
                        nc.vector.tensor_scalar(em2[:, t % 2, :], ex2[:, t % 2, :], 1.0, -1.0,
                                                ALU.min, ALU.add).then_inc(em2_ready, 1)
                        dve.wait_ge(em2_ready, b * TB + t + 1)
                        if due(b * TB + max(t - 1, 0)):
                            dve.wait_ge(x2_ready, b * TB + max(t - 1, 0))
                        nc.vector.tensor_tensor(z2[:, t % 2, :], s2[:, t % 2, :], em2[:, t % 2, :],
                                                ALU.max).then_inc(z2_ready, 1)
                    for t in range(TB):
                        dve.wait_ge(l2_done, b * TB + t + 1)
                        if due(b * TB + max(t - 1, 0)):
                            dve.wait_ge(z2_ready, b * TB + max(t - 1, 0))
                        nc.vector.tensor_tensor(s2[:, t % 2, :], L2[t % 2][:], b1bc[:], ALU.add).then_inc(s2_ready, 1)
                        if t:
                            finish(t - 1)
                    finish(TB - 1)

                nc.vector.tensor_scalar(rstd[:], mv[:, :, 1], EPS, None, ALU.add).then_inc(var_ready, 1)
                link(nc.vector.tensor_tensor(gap[:], top[:, :, 0], top[:, :, 1], ALU.subtract))
                link(nc.vector.tensor_tensor(lead[:], top[:, :, 0], mv[:, :, 0], ALU.subtract))
                dve.wait_ge(abs_small, 5)
                nc.vector.tensor_tensor(bounds[:, 0:1], bounds[:, 3:4], bounds[:, 4:5], ALU.add)
                nc.vector.tensor_tensor(bounds[:, 1:2], bounds[:, 5:6], bounds[:, 6:7], ALU.add)
                nc.vector.tensor_reduce(bounds[:, 2:3], small[:, 4, :], AX_X, ALU.max).then_inc(bounds_ready, 1)
                dve.wait_ge(abs_small, 6)
                nc.vector.tensor_reduce(rowstat[:, 0:1], ctx_all[:], AX_X, ALU.max)
                dve.wait_ge(rstd_ready, 1)
                link(nc.vector.tensor_tensor(gap[:], gap[:], rstd[:], ALU.mult))
                link(nc.vector.tensor_tensor(lead[:], lead[:], rstd[:], ALU.mult))
                link(nc.vector.scalar_tensor_tensor(lead[:], lead[:], -1.0, lead[:], ALU.mult, ALU.max))
                link(nc.vector.tensor_scalar(lead[:], lead[:], 1.0, 6e-7, ALU.add, ALU.mult))
                link(nc.vector.scalar_tensor_tensor(gap[:], gap[:], -0.99, lead[:], ALU.mult, ALU.add))
                nc.vector.tensor_reduce(rowstat[:, 1:2], gap[:], AX_X, ALU.max).then_inc(rows_ready, 1)
                dve.wait_ge(colsum_done, 1)
                nc.vector.tensor_reduce(colsum[:, 0:1], CS[0][:], AX_X, ALU.max)
                link(nc.vector.tensor_reduce(colsum[:, 1:2], CS[1][:], AX_X, ALU.max))
                dve.wait_ge(reduced, 2)
                f = fin
                link(nc.vector.tensor_tensor(f[:, 0:1], rowstat_max[0:1, 0:1], colsum[0:1, 0:1], ALU.mult))
                link(nc.vector.tensor_tensor(f[:, 1:2], f[:, 0:1], bounds_max[0:1, 2:3], ALU.add))
                link(nc.vector.tensor_tensor(f[:, 1:2], f[:, 1:2], colsum[0:1, 1:2], ALU.mult))
                link(nc.vector.tensor_tensor(f[:, 0:1], f[:, 0:1], bounds_max[0:1, 0:1], ALU.mult))
                link(nc.vector.scalar_tensor_tensor(f[:, 1:2], f[:, 1:2], bounds_max[0:1, 1:2], f[:, 0:1],
                                                    ALU.mult, ALU.add))
                link(nc.vector.tensor_scalar(f[:, 1:2], f[:, 1:2], -2.1 / MASK_VAL, -120.0 / MASK_VAL, ALU.mult, ALU.add))
                link(nc.vector.tensor_tensor(f[:, 2:3], f[:, 1:2], rowstat_max[0:1, 1:2], ALU.add))
                link(nc.vector.tensor_scalar(f[:, 3:4], f[:, 2:3], 0.0, -1.0, ALU.is_lt, ALU.mult))
                link(nc.vector.tensor_scalar(k.flag[:], f[:, 3:4], 1.0, None, ALU.add))
                if FORCE_GENERAL:
                    link(nc.vector.memset(k.flag[:], 1))


def general_block(nc, k, a):
    with ExitStack() as ctx:
        def sb(name, shape, dt=F32):
            return ctx.enter_context(nc.sbuf_tensor(name, shape, dt))

        loaded = ctx.enter_context(nc.semaphore("g_loaded"))
        nodes_in = ctx.enter_context(nc.semaphore("g_nodes_in"))
        g_passed = ctx.enter_context(nc.semaphore("g_passed"))
        xg = sb("g_x", [P, TB, D])
        cg = sb("g_ctx", [P, TB, FIN])
        bn = sb("g_bn", [P, TB, 6])
        mv = sb("g_mv", [P, TB, 2])
        rstd = sb("g_rstd", [P, TB])
        mhalf = sb("g_mhalf", [P, TB])
        mask = sb("g_mask", [P, TB, N])
        inT = sb("g_inT", [P, KC, N])
        feat = sb("g_feat", [P, TB, H * O])
        work = sb("g_work", [P, TB, N])
        attn = sb("g_attn", [P, 2, TB, H])
        diag = sb("g_diag", [P, TB, P])
        e = sb("g_e", [P, TB, N])
        pT = sb("g_pT", [P, TB, N])
        nmax = sb("g_nmax", [P, TB])
        total = sb("g_total", [P, TB])
        o = sb("g_o", [P, TB, H * O])
        w0 = sb("g_w0", [P, 1, H * O])
        w1 = sb("g_w1", [P, KC, H * O])
        avec = sb("g_avec", [P, 6, H * O])
        bank = k.psum

        def stage(vector=None, scalar=None, tensor=None, gpsimd=None, sync=None):
            with nc.Block() as block:
                if vector:
                    block.vector(lambda dve: vector())
                if scalar:
                    block.scalar(lambda act: scalar())
                if tensor:
                    block.tensor(lambda pe: tensor())
                if gpsimd:
                    block.gpsimd(lambda pool: gpsimd())
                if sync:
                    block.sync(sync)

        def flat(ap):
            return ap.rearrange("p t n -> p (t n)")

        def load_weights(sp):
            sp.dma_start(w0[:, 0, :].rearrange("f (h o) -> f h o", h=H), a["W0"].rearrange("h f o -> f h o")).then_inc(loaded, 16)
            for c in range(KC):
                sp.dma_start(w1[:, c, :].rearrange("f (h o) -> f h o", h=H),
                             a["W1"][:, c * P:(c + 1) * P, :].rearrange("h f o -> f h o")).then_inc(loaded, 16)
            for j, name in enumerate(("a_self0", "a_neigh0", "b0", "a_self1", "a_neigh1", "b1")):
                sp.dma_start(avec[:, j, :], a[name].rearrange("h o -> (h o)").rearrange("(u d) -> u d", u=1)
                             .broadcast_to([P, H * O])).then_inc(loaded, 16)
            sp.wait_ge(loaded, 16 * (1 + KC + 6))
        for engine in (nc.vector, nc.scalar, nc.tensor, nc.gpsimd, nc.sync):
            engine.sem_inc(g_passed, 1)
        stage(sync=load_weights, gpsimd=lambda: nc.gpsimd.memset(mhalf[:], -0.5))

        def each(f, n=TB):
            def run():
                for t in range(n):
                    f(t)
            return run

        def layer(chunks, w, at):
            def products():
                for t in range(TB):
                    for c in range(chunks):
                        nc.tensor.matmul(bank[t][:], inT[:, c, t * P:(t + 1) * P], w[:, c, :],
                                         start=(c == 0), stop=(c == chunks - 1))
            stage(tensor=products)
            stage(scalar=each(lambda t: nc.scalar.activation(feat[:, t, :], bank[t][:], ACT.Copy)))
            for j in range(2):
                stage(vector=each(lambda t: nc.vector.tensor_tensor(work[:, t, :], feat[:, t, :], avec[:, at + j, :], ALU.mult)))
                stage(vector=each(lambda t: nc.vector.tensor_reduce(
                    attn[:, j, t, :], work[:, t, :].rearrange("p (h o) -> p h o", h=H), AX_X, ALU.add)))
            with nc.Fori(0, H) as h:
                stage(vector=each(lambda t: nc.vector.tensor_scalar(
                    diag[:, t, :], k.ident[:], attn[:, 1, t, bass.ds(h, 1)], None, ALU.mult)))
                stage(tensor=each(lambda t: nc.tensor.matmul(bank[5][:, t * P:(t + 1) * P], k.ones[:], diag[:, t, :],
                                                             start=True, stop=True)))
                stage(vector=each(lambda t: nc.vector.tensor_scalar(
                    e[:, t, :], bank[5][:], attn[:, 0, t, bass.ds(h, 1)], None, ALU.add)))
                stage(vector=lambda: nc.vector.scalar_tensor_tensor(flat(work[:]), flat(e[:]), LRELU, flat(e[:]), ALU.mult, ALU.max))
                stage(vector=lambda: nc.vector.tensor_tensor(flat(e[:]), flat(work[:]), flat(mask[:]), ALU.add))
                stage(vector=lambda: nc.vector.tensor_reduce(nmax[:], e[:], AX_X, ALU.max))
                stage(vector=each(lambda t: nc.vector.tensor_scalar(work[:, t, :], e[:, t, :], nmax[:, t:t + 1], None, ALU.subtract)))
                stage(scalar=each(lambda t: nc.scalar.activation(e[:, t, :], work[:, t, :], ACT.Exp, accum_out=total[:, t:t + 1])))
                stage(tensor=each(lambda q: nc.tensor.transpose(bank[q // TB][:, (q % TB) * P:(q % TB + 1) * P],
                                                                e[:, q // TB, (q % TB) * P:(q % TB + 1) * P], k.ident[:]), TB * TB),
                      vector=lambda: nc.vector.reciprocal(nmax[:], total[:]))
                stage(scalar=each(lambda t: nc.scalar.activation(pT[:, t, :], bank[t][:], ACT.Copy)))

                def attend():
                    for t in range(TB):
                        for c in range(TB):
                            nc.tensor.matmul(bank[t][:, 0:O], pT[:, t, c * P:(c + 1) * P], feat[:, c, bass.ds(h * O, O)],
                                             start=(c == 0), stop=(c == TB - 1))
                stage(tensor=attend)
                stage(vector=each(lambda t: nc.vector.tensor_scalar(
                    o[:, t, bass.ds(h * O, O)], bank[t][:, 0:O], nmax[:, t:t + 1], None, ALU.mult)))
            stage(vector=each(lambda t: nc.vector.tensor_tensor(o[:, t, :], o[:, t, :], avec[:, at + 2, :], ALU.add)))
            stage(scalar=lambda: nc.scalar.activation(flat(work[:]), flat(o[:]), ACT.Exp))
            stage(vector=lambda: nc.vector.tensor_scalar(flat(work[:]), flat(work[:]), 1.0, -1.0, ALU.min, ALU.add))
            stage(vector=lambda: nc.vector.tensor_tensor(flat(o[:]), flat(o[:]), flat(work[:]), ALU.max))

        with nc.Fori(0, B) as b:
            def load(sp):
                sp.dma_start(xg[:], a["x"][bass.ds(b, 1)].rearrange("u (t p) d -> p (u t) d", p=P)).then_inc(nodes_in, 16)
                sp.dma_start(cg[:], a["ctx"][bass.ds(b * N, N), :].rearrange("(t p) f -> p t f", p=P)).then_inc(nodes_in, 16)
                sp.wait_ge(nodes_in, (b + 1) * 32)
                sp.sem_inc(g_passed, 1)
            stage(sync=load)
            stage(vector=each(lambda t: nc.vector.bn_stats(bn[:, t, :], xg[:, t, :])),
                  tensor=each(lambda t: nc.tensor.transpose(bank[0][:, t * P:(t + 1) * P], cg[:, t, :], k.ident[:])))
            stage(vector=each(lambda t: nc.vector.bn_aggr(mv[:, t, :], bn[:, t, :])),
                  scalar=lambda: nc.scalar.activation(inT[:, 0, :], bank[0][:], ACT.Copy))
            stage(vector=lambda: nc.vector.tensor_scalar(rstd[:], mv[:, :, 1], EPS, None, ALU.add))
            stage(gpsimd=lambda: nc.gpsimd.tensor_tensor(rstd[:], rstd[:], mhalf[:], ALU.pow))
            stage(vector=each(lambda t: nc.vector.tensor_scalar(work[:, t, :], xg[:, t, :], mv[:, t, 0:1], rstd[:, t:t + 1],
                                                                ALU.subtract, ALU.mult)))
            stage(vector=lambda: nc.vector.tensor_scalar(flat(mask[:]), flat(work[:]), -1.0, 1.0, ALU.mult, ALU.add))
            stage(vector=lambda: nc.vector.tensor_scalar(flat(mask[:]), flat(mask[:]), MASK_VAL, None, ALU.mult))
            layer(1, w0, 0)
            stage(tensor=each(lambda q: nc.tensor.transpose(bank[q // TB][:, (q % TB) * P:(q % TB + 1) * P],
                                                            o[:, q % TB, (q // TB) * P:(q // TB + 1) * P], k.ident[:]), KC * TB))
            stage(scalar=each(lambda c: nc.scalar.activation(inT[:, c, :], bank[c][:], ACT.Copy), KC))
            layer(KC, w1, 3)
            stage(vector=lambda: nc.vector.tensor_tensor(k.x[:, bass.ds(b * TB, TB), :], xg[:], o[:], ALU.add))


def experts_block(nc, k, a):
    with ExitStack() as ctx:
        def sb(name, shape, dt=F32):
            return ctx.enter_context(nc.sbuf_tensor(name, shape, dt))

        def sem(name):
            return ctx.enter_context(nc.semaphore(name))

        bank = k.psum
        gate_raw = sb("gate_raw", [E, D])
        gateT = sb("gateT", [P, KC, E])
        upT = sb("upT", [P, KC, 2 * SI])
        downT = sb("downT", [P, SC, D])
        bn = sb("bn_c", [P, TB, 6])
        mv = sb("mv_c", [P, TB, 2])
        rstd = sb("rstd_c", [P, TB])
        mhalf = sb("mhalf_c", [P, TB])
        rows = sb("rows", [P, TB, ROW])
        rowsT = sb("rowsT", [P, KC, N])
        xnT = sb("xnT", [P, KC, T])
        raw_all = xnT[:].rearrange("p c t -> p (c t)")
        raw = raw_all[:, 0:2 * SC * D].rearrange("p (s d) -> p s d", d=D)
        raw_down = raw_all[:, 2 * SC * D:2 * SC * D + KC * SI].rearrange("p (c s) -> p c s", s=SI)
        top = sb("top_c", [P, TB, 8])
        nmax = sb("nmax", [P, TB])
        lg = sb("lg", [P, TB, E])
        ex = sb("ex", [P, TB, E])
        esum = sb("esum", [P, TB])
        rsum = sb("rsum", [P, TB])
        key = sb("key", [P, TB, E])
        ktop = sb("ktop", [P, TB, 8])
        kix = sb("kix", [P, TB, 8], U32)
        kixf = sb("kixf", [P, TB, 8])
        krep = sb("krep", [P, TB, E])
        iota_e = sb("iota_e", [P, E])
        iota_ei = sb("iota_ei", [P, E], I32)
        left = sb("left", [P, NT * E])
        order_i = sb("order_i", [P, HALF], I32)
        order = sb("order", [P, HALF])
        val = sb("val", [P, HALF])
        cand = sb("cand", [P, CAP])
        both = sb("both", [E, 2 * CAP])
        slots = sb("slots", [E, CAP])
        late = sb("late", [E, CAP])
        table = sb("table", [P, E], U32)
        sg = sb("sg", [P, 2, N])
        shid = sb("shid", [P, SC, N])
        gu_w = sb("gu_w", [P, U, KC, 2 * I])
        dn_w = sb("dn_w", [IH, U, 2, D])
        gx = sb("gx", [P, U, ROW])
        gxT = sb("gxT", [P, 2, KC, P])
        slot_w = sb("slot_w", [P, 2, 1])
        eg = sb("eg", [P, I])
        hid = sb("hid", [P, 2, IH])
        hidT = sb("hidT", [IH, 2, 2, P])
        y = sb("y", [P, 2, D])
        idx_g = sb("idx_g", [P, U, 1], U32)
        idx_s = sb("idx_s", [P, 2, 1], U32)

        raw_in, wT_done, wT_sb = sem("raw_in"), sem("wT_done"), sem("wT_sb")
        lg_ready = sem("lg_ready")
        cc, vch = sem("cc"), sem("vch_c")
        dve_passed, pool_passed = sem("dve_passed"), sem("pool_passed")
        var_ready, rstd_ready, xn_ready, xT_done, xT_sb, xnT_copied = (
            sem(s) for s in ("var_ready_c", "rstd_ready_c", "xn_ready", "xT_done", "xT_sb", "xnT_copied"))
        logits, nmax_ready, exp_done, rows_full, rows_out, left_ready, leftT_done, val_ready = (
            sem(s) for s in ("logits", "nmax_ready", "exp_done", "rows_full", "rows_out", "left_ready", "leftT_done", "val_ready"))
        cand_ready, both_in, slots_ready, slotsT_done, table_ready = (
            sem(s) for s in ("cand_ready", "both_in", "slots_ready", "slotsT_done", "table_ready"))
        sup_done, sg_ready, shid_ready, sdn_done, x3_ready, x3_out = (
            sem(s) for s in ("sup_done", "sg_ready", "shid_ready", "sdn_done", "x3_ready", "x3_out"))
        w_in = [sem(f"ew_in{u}") for u in range(U)]
        g_in = [sem(f"eg_in{u}") for u in range(U)]
        pidx, gT_done, gxT_ready, w_copied, gu_done, eg_ready, hid_ready, hT_done, hidT_ready, dn_done, y_ready, y_free, scat = (
            sem(s) for s in ("pidx", "egT_done", "gxT_ready", "w_copied", "gu_done", "eg_ready", "hid_ready",
                             "hT_done", "hidT_ready", "dn_done", "y_ready", "y_free", "scat"))

        wt = []
        for c in range(KC):
            wt.append(([gate_raw[:, :].rearrange("e (p c) -> e c p", c=KC)[:, c, :]], E, gateT[:, c, :]))
        for c in range(KC):
            for g in range(2):
                wt.append(([raw[:, g * SC + s, :].rearrange("q (p c) -> q c p", c=KC)[:, c, :] for s in range(SC)],
                           P, upT[:, c, g * SI:(g + 1) * SI]))
        for s in range(SC):
            wt.append(([raw_down[:, c, s * P:(s + 1) * P] for c in range(KC)], P, downT[:, s, :]))
        WB = 2
        XT, LG = bank[2], bank[3]

        with nc.Block() as block:
            def load_expert(sp, e, u):
                def of(name):
                    w = a[name]
                    return w[e] if isinstance(e, int) else w[bass.ds(e, 1)].rearrange("u r n -> (u r) n")
                sp.dma_start(gu_w[:, u, :, :], of("gate_up").rearrange("(p c) n -> p c n", c=KC)).then_inc(w_in[u], 16)
                sp.dma_start(dn_w[:, u, :, :], of("down").rearrange("(p j) n -> p j n", j=2)).then_inc(w_in[u], 16)

            @block.sync
            def _(sp):
                sp.dma_start(gate_raw[:], a["gate_w"]).then_inc(raw_in, 16)
                sp.dma_start(raw[:, 0:SC, :], a["sh_gate"].rearrange("(s p) d -> p s d", p=P)).then_inc(raw_in, 16)
                sp.dma_start(raw[:, SC:2 * SC, :], a["sh_up"].rearrange("(s p) d -> p s d", p=P)).then_inc(raw_in, 16)
                sp.dma_start(raw_down, a["sh_down"].rearrange("(c p) s -> p c s", p=P)).then_inc(raw_in, 16)
                for u in range(U):
                    load_expert(sp, u, u)
                for b in range(B):
                    sp.wait_ge(rows_full, b + 1)
                    sp.dma_start(a["rows_dram"][b * N:(b + 1) * N, :].rearrange("(t p) r -> p t r", p=P),
                                 rows[:]).then_inc(rows_out, 16)
                sp.wait_ge(cand_ready, 1)
                sp.dma_start(both[:, 0:CAP], cand[0:E, :]).then_inc(both_in, 16)
                sp.dma_start(both[:, CAP:2 * CAP], cand[E:2 * E, :]).then_inc(both_in, 16)
                for b in range(B):
                    sp.wait_ge(x3_ready, (b + 1) * TB)
                    sp.dma_start(a["out"][b * N:(b + 1) * N, :].rearrange("(t p) d -> p t d", p=P),
                                 k.x[:, b * TB:(b + 1) * TB, :]).then_inc(x3_out, 16)
                with sp.Fori(1, E // U) as i:
                    for u in range(U):
                        sp.wait_ge(dn_done, (i - 1) * U + u + 1)
                        load_expert(sp, i * U + u, u)

            @block.gpsimd
            def _(pool):
                nc.gpsimd.memset(mhalf[:], -0.5)
                nc.gpsimd.iota(iota_ei[:], pattern=[[1, E]], base=0, channel_multiplier=0).then_inc(cc, 1)
                for u in range(2):
                    pool.wait_ge(cc, u + 1)
                    nc.gpsimd.iota(order_i[u * E:(u + 1) * E, :], pattern=[[-2 * P, NT // 2], [-1, P]],
                                   base=3 * T - u * P, channel_multiplier=0).then_inc(cc, 1)
                pool.wait_ge(cc, 3)
                nc.gpsimd.tensor_copy(iota_e[:], iota_ei[:])
                nc.gpsimd.tensor_copy(order[:], order_i[:]).then_inc(cc, 1)
                for b in turns(pool, B):
                    pool.wait_ge(var_ready, b + 1)
                    nc.gpsimd.tensor_tensor(rstd[:], rstd[:], mhalf[:], ALU.pow).then_inc(rstd_ready, 1)
                    pool.wait_ge(xT_sb, (b + 1) * TB)
                    nc.gpsimd.tensor_copy(xnT[:, :, bass.ds(b * N, N)], rowsT[:]).then_inc(xnT_copied, 1)

                def scatter(e, u):
                    if not (isinstance(e, int) and e == 0):
                        if due(e * 16):
                            pool.wait_ge(scat, e * 16)
                        pool.sem_inc(pool_passed, 1)
                    nc.gpsimd.tensor_copy(idx_s[:, u % 2, :], table[:, bass.ds(e, 1)]).then_inc(y_free, 1)
                    pool.wait_ge(y_free, e + 1)
                    pool.wait_ge(y_ready, e + 1)
                    pool.sem_inc(pool_passed, 1)
                    pool.indirect_dma_start(a["out"][:, :], bass.IndirectOffsetOnAxis(ap=idx_s[:, u % 2, :], axis=0),
                                            y[:, u % 2, :], None, compute_op=ALU.add).then_inc(scat, 16)

                pool.wait_ge(table_ready, 1)
                pool.wait_ge(rows_out, 16 * B)
                pool.wait_ge(x3_out, 16 * B)
                for e in range(U - 1):
                    nc.gpsimd.tensor_copy(idx_g[:, e, :], table[:, e:e + 1]).then_inc(pidx, 1)
                    pool.wait_ge(pidx, e + 1)
                    pool.indirect_dma_start(gx[:, e, :], None, a["rows_dram"][:, :],
                                            bass.IndirectOffsetOnAxis(ap=idx_g[:, e, :], axis=0)).then_inc(g_in[e], 16)

                def gather_ahead(n, i, u):
                    e, s = n + U - 1, (u + U - 1) % U
                    if not (isinstance(n, int) and n == 0):
                        if due(n):
                            pool.wait_ge(gT_done, n)
                        if due(n):
                            pool.wait_ge(w_copied, n)
                        pool.sem_inc(pool_passed, 1)
                    nc.gpsimd.tensor_copy(idx_g[:, s, :], table[:, bass.ds(e, 1)]).then_inc(pidx, 1)
                    pool.wait_ge(pidx, n + U)
                    pool.sem_inc(pool_passed, 1)
                    pool.indirect_dma_start(gx[:, s, :], None, a["rows_dram"][:, :],
                                            bass.IndirectOffsetOnAxis(ap=idx_g[:, s, :], axis=0)).then_inc(g_in[s], 16)

                def turn(i, last):
                    for u in range(U):
                        n = i * U + u
                        if not (last and u > 0):
                            gather_ahead(n, i, u)
                        scatter(n, u)
                for i in turns(pool, E // U - 1):
                    turn(i, False)
                turn(E // U - 1, True)
                pool.wait_ge(scat, 16 * E)

            @block.tensor
            def _(pe):
                pe.wait_ge(raw_in, 64)
                for j, (parts, r, dst) in enumerate(wt):
                    if j >= WB:
                        pe.wait_ge(wT_sb, j - WB + 1)
                    for q, src in enumerate(parts):
                        last = nc.tensor.transpose(bank[j % WB][:, q * r:(q + 1) * r], src, k.ident[0:r, 0:r])
                    last.then_inc(wT_done, 1)
                pe.wait_ge(wT_sb, len(wt))
                for b in turns(pe, B):
                    for t in range(TB):
                        pe.wait_ge(xn_ready, b * TB + t + 1)
                        if due(b * TB + t):
                            pe.wait_ge(xT_sb, b * TB + t)
                        for c in range(KC):
                            last = nc.tensor.transpose(XT[:, c * P:(c + 1) * P], rows[:, t, c * P:(c + 1) * P], k.ident[:])
                        last.then_inc(xT_done, 1)
                    for t in range(TB):
                        pe.wait_ge(xT_sb, b * TB + t + 1)
                        if t == 0:
                            if due(b):
                                pe.wait_ge(lg_ready, b)
                        for c in range(KC):
                            last = nc.tensor.matmul(LG[:, t * E:(t + 1) * E], rowsT[:, c, t * P:(t + 1) * P], gateT[:, c, :],
                                                    start=(c == 0), stop=(c == KC - 1))
                    last.then_inc(logits, 1)
                pe.wait_ge(left_ready, B)
                pe.wait_ge(wT_sb, len(wt))
                for j in range(NT // 2):
                    last = nc.tensor.transpose(bank[j // 4][:, (j % 4) * P:(j % 4 + 1) * P],
                                               left[:, j * 2 * E:(j + 1) * 2 * E], k.ident[:])
                    if j % 4 == 3:
                        last.then_inc(leftT_done, 1)
                pe.wait_ge(xnT_copied, B)
                for b in turns(pe, B):
                    for s in range(SC):
                        if due(b * SC + s):
                            pe.wait_ge(sg_ready, b * SC + s)
                        if due(b * SC + s):
                            pe.wait_ge(shid_ready, b * SC + s)
                        for g in range(2):
                            for c in range(KC):
                                last = nc.tensor.matmul(bank[5 + g][:], upT[:, c, g * SI + s * P:g * SI + (s + 1) * P],
                                                        xnT[:, c, bass.ds(b * N, N)], start=(c == 0), stop=(c == KC - 1))
                            last.then_inc(sup_done, 1)
                    for t in range(TB):
                        pe.wait_ge(shid_ready, (b + 1) * SC)
                        if due(b * TB + t):
                            pe.wait_ge(x3_ready, b * TB + t)
                        for s in range(SC):
                            last = nc.tensor.matmul(bank[7][:], shid[:, s, t * P:(t + 1) * P], downT[:, s, :],
                                                    start=(s == 0), stop=(s == SC - 1))
                        last.then_inc(sdn_done, 1)
                pe.wait_ge(slots_ready, 1)
                nc.tensor.transpose(bank[2][:, 0:E], slots[:], k.ident[0:E, 0:E]).then_inc(slotsT_done, 1)

                GT, GU, HT, DN = bank[0:2], bank[3:5], bank[5], bank[6]

                def transposes(n, u, i1):
                    pe.wait_ge(g_in[u % U], 16 * i1)
                    for c in range(KC):
                        last = nc.tensor.transpose(GT[u % 2][:, c * P:(c + 1) * P], gx[:, u % U, c * P:(c + 1) * P], k.ident[:])
                    last.then_inc(gT_done, 1)

                def down(n, u):
                    pe.wait_ge(hidT_ready, n + 1)
                    if due(n):
                        pe.wait_ge(y_ready, n)
                    for j in range(2):
                        last = nc.tensor.matmul(DN[:], hidT[:, u % 2, j, :], dn_w[:, u % U, j, :],
                                                start=(j == 0), stop=(j == 1))
                    last.then_inc(dn_done, 1)

                def step(i, u, first, last_step):
                    n = i * U + u
                    pe.wait_ge(w_in[u], (i + 1) * 32)
                    pe.wait_ge(gxT_ready, n + 1)
                    for c in range(KC):
                        last = nc.tensor.matmul(GU[u % 2][:, 0:2 * I], gxT[:, u % 2, c, :], gu_w[:, u, c, :],
                                                start=(c == 0), stop=(c == KC - 1))
                    last.then_inc(gu_done, 1)
                    if not last_step:
                        transposes(n + 1, u + 1, i + 1 + (u + 1) // U)
                    if not first:
                        down(n - 1, (u - 1) % U)
                    pe.wait_ge(hid_ready, n + 1)
                    for j in range(2):
                        last = nc.tensor.transpose(HT[0:IH, j * P:(j + 1) * P], hid[:, j, :], k.ident[:])
                    last.then_inc(hT_done, 1)

                pe.wait_ge(table_ready, 1)
                pe.wait_ge(x3_ready, NT)
                transposes(0, 0, 1)
                for u in range(U):
                    step(0, u, u == 0, False)
                with pe.Fori(1, E // U - 1) as i:
                    for u in range(U):
                        step(i, u, False, False)
                for u in range(U):
                    step(E // U - 1, u, False, u == U - 1)
                down(E - 1, U - 1)

            @block.scalar
            def _(act):
                for j, (parts, r, dst) in enumerate(wt):
                    act.wait_ge(wT_done, j + 1)
                    nc.scalar.activation(dst, bank[j % WB][:, 0:r * len(parts)], ACT.Copy).then_inc(wT_sb, 1)
                for b in turns(act, B):
                    for t in range(TB):
                        act.wait_ge(xT_done, b * TB + t + 1)
                        if t == 0:
                            if due(b):
                                act.wait_ge(logits, b)
                            if due(b):
                                act.wait_ge(xnT_copied, b)
                        nc.scalar.activation(rowsT[:, :, t * P:(t + 1) * P], XT[:].rearrange("p (c q) -> p c q", c=KC),
                                             ACT.Copy).then_inc(xT_sb, 1)
                    act.wait_ge(nmax_ready, b + 1)
                    if due(b):
                        act.wait_ge(rows_full, b)
                    for t in range(TB):
                        last = nc.scalar.activation(ex[:, t, :], lg[:, t, :], ACT.Exp, bias=nmax[:, t:t + 1],
                                                    accum_out=esum[:, t:t + 1])
                    last.then_inc(exp_done, 1)
                for b in turns(act, B):
                    for s in range(SC):
                        act.wait_ge(sup_done, b * (2 * SC) + 2 * s + 1)
                        if due(b * SC + s):
                            act.wait_ge(shid_ready, b * SC + s)
                        nc.scalar.activation(sg[:, 0, :], bank[5][:], ACT.Silu).then_inc(sg_ready, 1)

                def gx_copy(n, u):
                    act.wait_ge(gT_done, n + 1)
                    nc.scalar.activation(gxT[:, u % 2, :, :].rearrange("p c q -> p (c q)"), bank[u % 2][:],
                                         ACT.Copy).then_inc(gxT_ready, 1)

                def step(i, u, last_step):
                    n = i * U + u
                    act.wait_ge(gu_done, n + 1)
                    if due(n):
                        act.wait_ge(hid_ready, n)
                    nc.scalar.activation(eg[:], bank[3 + u % 2][:, 0:I], ACT.Silu).then_inc(eg_ready, 1)
                    if not last_step:
                        gx_copy(n + 1, u + 1)
                gx_copy(0, 0)
                for i in turns(act, E // U - 1):
                    for u in range(U):
                        step(i, u, False)
                for u in range(U):
                    step(E // U - 1, u, u == U - 1)

            @block.vector
            def _(dve):
                dve.wait_ge(cc, 4)
                LINKS = 10

                for b in turns(dve, B):
                    chain = [0]

                    def alone():
                        dve.wait_ge(cc, 4)

                    def link(ins, apart=False):
                        chain[0] += 1
                        ins.then_inc(vch, 1)
                        if apart:
                            dve.wait_ge(vch, b * LINKS + chain[0])
                            dve.sem_inc(dve_passed, 1)
                        else:
                            dve.wait_ge(vch, b * LINKS + chain[0])
                    for t in range(TB):
                        last = nc.vector.bn_stats(bn[:, t, :], k.x[:, bass.ds(b * TB + t, 1), :].rearrange("p u d -> p (u d)"))
                    link(last, apart=True)
                    for t in range(TB):
                        last = nc.vector.bn_aggr(mv[:, t, :], bn[:, t, :])
                    link(last)
                    nc.vector.tensor_scalar(rstd[:], mv[:, :, 1], EPS, None, ALU.add).then_inc(var_ready, 1)
                    dve.wait_ge(rstd_ready, b + 1)
                    if due(b * 16):
                        dve.wait_ge(rows_out, b * 16)
                    for t in range(TB):
                        nc.vector.tensor_scalar(
                            rows[:, t, 0:D].rearrange("q (c p) -> q c p", c=KC),
                            k.x[:, bass.ds(b * TB + t, 1), :].rearrange("q u (p c) -> q (u c) p", c=KC),
                            mv[:, t, 0:1], rstd[:, t:t + 1], ALU.subtract, ALU.mult).then_inc(xn_ready, 1)
                    dve.wait_ge(logits, b + 1)
                    dve.sem_inc(dve_passed, 1)
                    if due(b):
                        dve.wait_ge(exp_done, b)
                    nc.vector.tensor_copy(lg[:].rearrange("p t e -> p (t e)"), LG[:, 0:TB * E]).then_inc(lg_ready, 1)
                    dve.wait_ge(lg_ready, b + 1)
                    dve.sem_inc(dve_passed, 1)
                    for t in range(TB):
                        last = nc.vector.max(top[:, t, :], lg[:, t, :])
                    link(last)
                    nc.vector.tensor_scalar(nmax[:], top[:, :, 0], -1.0, None, ALU.mult).then_inc(nmax_ready, 1)
                    for t in range(TB):
                        last = nc.vector.tensor_scalar(key[:, t, :], lg[:, t, :], top[:, t, 0:1], EXP_FLOOR,
                                                       ALU.subtract, ALU.max)
                    link(last, apart=True)
                    for t in range(TB):
                        last = nc.vector.max(ktop[:, t, :], key[:, t, :])
                    link(last, apart=True)
                    for t in range(TB):
                        nc.vector.match_replace(krep[:, t, :], ktop[:, t, :], key[:, t, :], -1000.0)
                        last = nc.vector.max_index(kix[:, t, :], ktop[:, t, :], key[:, t, :])
                    link(last)
                    nc.vector.tensor_copy(kixf[:], kix[:])
                    link(nc.vector.tensor_scalar(krep[:], krep[:], -500.0, None, ALU.is_gt))
                    for j in (TOPK, TOPK + 1):
                        for t in range(TB):
                            last = nc.vector.scalar_tensor_tensor(krep[:, t, :], iota_e[:], kixf[:, t, j:j + 1],
                                                                  krep[:, t, :], ALU.is_equal, ALU.add)
                        link(last)
                    dve.wait_ge(exp_done, b + 1)
                    nc.vector.tensor_copy(left[:, bass.ds(b * (TB * E), TB * E)],
                                          krep[:].rearrange("p t e -> p (t e)")).then_inc(left_ready, 1)
                    nc.vector.reciprocal(rsum[:], esum[:])
                    link(nc.vector.scalar_tensor_tensor(ex[:], krep[:], 0.0, ex[:], ALU.is_equal, ALU.mult))
                    for t in range(TB):
                        last = nc.vector.tensor_scalar(rows[:, t, D:ROW], ex[:, t, :], rsum[:, t:t + 1], None, ALU.mult)
                    last.then_inc(rows_full, 1)
                    dve.wait_ge(rows_full, b + 1)
                    assert chain[0] == LINKS, chain[0]

                base = B * LINKS
                chain = [0]

                def link2(ins):
                    chain[0] += 1
                    ins.then_inc(vch, 1)
                    dve.wait_ge(vch, base + chain[0])
                for q in range(2):
                    dve.wait_ge(leftT_done, q + 1)
                    link2(nc.vector.scalar_tensor_tensor(val[:, q * 512:(q + 1) * 512], bank[q][:], -2.0 * T,
                                                         order[:, q * 512:(q + 1) * 512], ALU.mult, ALU.add))

                shared = [0]

                def shared_up(b, s):
                    dve.wait_ge(sup_done, b * (2 * SC) + 2 * s + 2)
                    dve.wait_ge(sg_ready, b * SC + s + 1)
                    if s == 0:
                        if due(b * TB):
                            dve.wait_ge(sdn_done, b * TB)
                    nc.vector.tensor_tensor(shid[:, s, :], bank[6][:], sg[:, 0, :], ALU.mult).then_inc(shid_ready, 1)

                def shared_down(b, t):
                    dve.wait_ge(sdn_done, b * TB + t + 1)
                    xs = k.x[:, b * TB + t, :] if isinstance(b, int) else k.x[:, bass.ds(b * TB + t, 1), :].rearrange("p u d -> p (u d)")
                    nc.vector.tensor_tensor(xs, bank[7][:], xs, ALU.add).then_inc(x3_ready, 1)

                def extract(r):
                    link2(nc.vector.max(cand[:, r * 8:(r + 1) * 8], val[:]))
                    link2(nc.vector.match_replace(val[:], cand[:, r * 8:(r + 1) * 8], val[:], 0.0))
                R = CAP // 8
                done = 0
                for b in range(B):
                    for s in range(SC):
                        if b < 3:
                            for r in range(done, min(done + 2, R)):
                                extract(r)
                            done = min(done + 2, R)
                            if done == R and s == 1 and b == 2:
                                pass
                        shared_up(b, s)
                    if b == 2:
                        while done < R:
                            extract(done)
                            done += 1
                    for t in range(TB):
                        shared_down(b, t)
                nc.vector.tensor_copy(bn[:, 0, 0:1], bn[:, 0, 0:1]).then_inc(cand_ready, 1)
                dve.wait_ge(both_in, 32)
                for r in range(R):
                    link2(nc.vector.max(slots[:, r * 8:(r + 1) * 8], both[:]))
                    if r < R - 1:
                        link2(nc.vector.match_replace(both[:], slots[:, r * 8:(r + 1) * 8], both[:], 0.0))
                link2(nc.vector.tensor_scalar(late[:], slots[:], float(T) + 0.5, 2.0 * T, ALU.is_gt, ALU.mult))
                link2(nc.vector.scalar_tensor_tensor(late[:], late[:], float(T), slots[:], ALU.add, ALU.subtract))
                nc.vector.tensor_copy(slots[:], late[:]).then_inc(slots_ready, 1)
                dve.wait_ge(slotsT_done, 1)
                nc.vector.tensor_copy(table[:], bank[2][:, 0:E]).then_inc(table_ready, 1)

                def scaled(n, u):
                    dve.wait_ge(dn_done, n + 1)
                    dve.wait_ge(y_free, n + 1)
                    nc.vector.tensor_scalar(y[:, u % 2, :], bank[6][:], slot_w[:, u % 2, :], None, ALU.mult).then_inc(y_ready, 1)

                def step(i, u, first):
                    n = i * U + u
                    dve.wait_ge(gT_done, n + 1)
                    if not (isinstance(n, int) and n < 2):
                        if due(n - 1):
                            dve.wait_ge(y_ready, n - 1)
                    nc.vector.tensor_copy(slot_w[:, u % 2, :], gx[:, u, bass.ds(n + D, 1)]).then_inc(w_copied, 1)
                    dve.wait_ge(eg_ready, n + 1)
                    if due(n):
                        dve.wait_ge(hT_done, n)
                    nc.vector.tensor_tensor(hid[:].rearrange("s j p -> s p j"), bank[3 + u % 2][:, I:2 * I].rearrange("s (p j) -> s p j", j=2),
                                            eg[:].rearrange("s (p j) -> s p j", j=2), ALU.mult).then_inc(hid_ready, 1)
                    if not first:
                        scaled(n - 1, (u - 1) % U)
                    dve.wait_ge(hT_done, n + 1)
                    nc.vector.tensor_copy(hidT[:, u % 2, :, :].rearrange("p j q -> p (j q)"), bank[5][0:IH, 0:2 * P]).then_inc(hidT_ready, 1)
                for u in range(U):
                    step(0, u, u == 0)
                with dve.Fori(1, E // U) as i:
                    for u in range(U):
                        step(i, u, False)
                scaled(E - 1, U - 1)


def build(nc, a):
    k = Kernel()
    with ExitStack() as ctx:
        allocate(nc, ctx, k)
        attention_block(nc, k, a)
        flag = nc.values_load(k.flag[0:1, 0:1], min_val=0, max_val=1)
        with nc.If(flag > 0):
            general_block(nc, k, a)
        nc.end_ifs()
        experts_block(nc, k, a)


_INS = {"x": "x", "ctx_512": "ctx", "L0_xattn_W0": "W0", "L0_xattn_a_self0": "a_self0",
        "L0_xattn_a_neigh0": "a_neigh0", "L0_xattn_b0": "b0", "L0_xattn_W1": "W1",
        "L0_xattn_a_self1": "a_self1", "L0_xattn_a_neigh1": "a_neigh1", "L0_xattn_b1": "b1",
        "L0_ffn_gate_w": "gate_w", "L0_ffn_gate_up_proj": "gate_up", "L0_ffn_down_proj": "down",
        "L0_ffn_shared_gate_w": "sh_gate", "L0_ffn_shared_up_w": "sh_up", "L0_ffn_shared_down_w": "sh_down"}


def kernel(**inputs):
    import numpy as _np
    import concourse.bacc as _bacc
    from concourse.bass_utils import run_bass_kernel_spmd as _run

    nc = _bacc.Bacc("TRN2", target_bir_lowering=False, num_devices=1)
    arrays, a = {}, {}
    for name, short in _INS.items():
        v = _np.ascontiguousarray(inputs[name])
        if short == "ctx":
            v = v.reshape(T, FIN)
        arrays[f"in_{short}"] = v
        a[short] = nc.dram_tensor(f"in_{short}", v.shape, mybir.dt.from_np(v.dtype), kind="ExternalInput").ap()
    a["out"] = nc.dram_tensor("out", (T, D), F32, kind="ExternalOutput").ap()
    a["node_dram"] = nc.dram_tensor("node_dram", (T, 1), U32, kind="Internal").ap()
    a["rows_dram"] = nc.dram_tensor("rows_dram", (T, ROW), F32, kind="Internal").ap()
    build(nc, a)
    r = _run(nc, [arrays], core_ids=[0])
    return r.results[0]["out"].reshape(B, N, D)
```

```python
from contextlib import ExitStack

import concourse.bass as bass
import concourse.mybir as mybir

F32 = mybir.dt.float32
U32 = mybir.dt.uint32
I32 = mybir.dt.int32
ALU = mybir.AluOpType
ACT = mybir.ActivationFunctionType
AX_X = mybir.AxisListType.X
RMAX = bass.bass_isa.ReduceOp.max

P = 128
B, N, D = 4, 512, 512
FIN, H, O = 128, 8, 64
T = B * N
NT = T // P
TB = N // P
KC = D // P
E, TOPK, CAP = 64, 6, 128
I = 192
IH = I // 2
SI = 2 * I
SC = SI // P
ROW = D + E
EPS = 1e-5
LRELU = 0.2
MASK_VAL = -1e10
U = 4
EXP_FLOOR = -87.336
HALF = T // 2
FORCE_GENERAL = False


def due(value):
    return not (isinstance(value, int) and value <= 0)


def turns(engine, n):
    yield 0
    with engine.Fori(1, n) as i:
        yield i




class Kernel:
    pass


def allocate(nc, ctx, k):
    def sb(name, shape, dt=F32):
        return ctx.enter_context(nc.sbuf_tensor(name, shape, dt))

    k.x = sb("x", [P, NT, D])
    k.ident = sb("ident", [P, P])
    k.ones = sb("ones", [P, P])
    k.flag = sb("flag", [1, 1], I32)
    k.psum = [ctx.enter_context(nc.psum_tensor(f"bank{i}", [P, 512], F32)) for i in range(8)]


def attention_block(nc, k, a):
    with ExitStack() as ctx:
        def sb(name, shape, dt=F32):
            return ctx.enter_context(nc.sbuf_tensor(name, shape, dt))

        def sem(name):
            return ctx.enter_context(nc.semaphore(name))

        w0 = sb("w0", [P, H * O])
        w1 = sb("w1", [P, KC, H * O])
        absw = sb("absw", [P, KC + 1, H * O])
        b0t = sb("b0t", [P, KC])
        b1bc = sb("b1bc", [P, H * O])
        ctx_all = sb("ctx_all", [P, NT * FIN])
        small = sb("small", [H, 5, O])
        bounds = sb("bounds", [H, 8])
        bounds_max = sb("bounds_max", [H, 4])
        rowstat = sb("rowstat", [P, 2])
        rowstat_max = sb("rowstat_max", [P, 2])
        colsum = sb("colsum", [P, 2])
        fin = sb("fin", [1, 8])
        top = sb("top", [P, NT, 8])
        top_ix = sb("top_ix", [P, NT, 8], U32)
        node = sb("node", [P, NT], U32)
        node2 = sb("node2", [P, NT], U32)
        bn = sb("bn", [P, NT, 6])
        mv = sb("mv", [P, NT, 2])
        rstd = sb("rstd", [P, NT])
        gap = sb("gap", [P, NT])
        lead = sb("lead", [P, NT])
        mhalf = sb("mhalf", [P, NT])
        gath = sb("gath", [P, 2, TB, FIN])
        gathT = sb("gathT", [P, 2, N])
        h1T = sb("h1T", [P, 2, KC, N])
        ex1 = sb("ex1", [P, 2, N])
        em1 = sb("em1", [P, 2, N])
        s2 = sb("s2", [P, 2, H * O])
        ex2 = sb("ex2", [P, 2, H * O])
        em2 = sb("em2", [P, 2, H * O])
        z2 = sb("z2", [P, 2, H * O])

        x_in = [sem(f"x_in{b}") for b in range(B)]
        w_in, small_in, w1_in, ctx_in = sem("w_in"), sem("small_in"), sem("w1_in"), sem("ctx_in")
        consts = sem("consts")
        vch = sem("vch")
        node_ready, node_stored, node2_in = (sem(s) for s in ("node_ready", "node_stored", "node2_in"))
        gath_in = [sem(f"gath_in{j}") for j in range(2)]
        bn_ready = sem("bn_ready")
        gT_done, gT_sb = sem("gT_done"), sem("gT_sb")
        l1_done, l1_exp, l1_em, h1_ready = (sem(s) for s in ("l1_done", "l1_exp", "l1_em", "h1_ready"))
        l2_done, s2_ready, l2_exp, em2_ready, z2_ready, x2_ready = (sem(s) for s in ("l2_done", "s2_ready", "l2_exp", "em2_ready", "z2_ready", "x2_ready"))
        absw_done, colsum_done, abs_small, bounds_ready, reduced, rstd_ready, var_ready, rows_ready = (
            sem(s) for s in ("absw_done", "colsum_done", "abs_small", "bounds_ready", "reduced", "rstd_ready", "var_ready", "rows_ready"))
        pch = sem("pch")

        bank = k.psum
        GT, L1, L2 = bank[0], bank[1:3], bank[3:5]
        CS = bank[5:7]

        with nc.Block() as block:
            @block.sync
            def _(sp):
                for b in range(B):
                    sp.dma_start(k.x[:, b * TB:(b + 1) * TB, :],
                                 a["x"][b].rearrange("(t p) d -> p t d", p=P)).then_inc(x_in[b], 16)
                    if b == 0:
                        sp.dma_start(w0[:].rearrange("f (h o) -> f h o", h=H),
                                     a["W0"].rearrange("h f o -> f h o")).then_inc(w_in, 16)
                        sp.dma_start(b0t[:], a["b0"].rearrange("h o -> (h o)").rearrange("(c p) -> p c", p=P),
                                     allow_slow_non_contiguous=True).then_inc(w_in, 16)
                for c in range(KC):
                    sp.dma_start(w1[:, c, :].rearrange("f (h o) -> f h o", h=H),
                                 a["W1"][:, c * P:(c + 1) * P, :].rearrange("h f o -> f h o")).then_inc(w1_in, 16)
                sp.dma_start(b1bc[:], a["b1"].rearrange("h o -> (h o)").rearrange("(u d) -> u d", u=1)
                             .broadcast_to([P, H * O])).then_inc(w1_in, 16)
                for j, name in enumerate(("a_self0", "a_neigh0", "a_self1", "a_neigh1", "b0")):
                    sp.dma_start(small[:, j, :], a[name]).then_inc(small_in, 16)
                sp.dma_start(ctx_all[:].rearrange("p (r f) -> p r f", f=FIN),
                             a["ctx"].rearrange("(p r) f -> p r f", p=P)).then_inc(ctx_in, 16)

            @block.gpsimd
            def _(pool):
                nc.gpsimd.memset(k.ident[:], 0.0).then_inc(pch, 1)
                pool.wait_ge(pch, 1)
                nc.gpsimd.affine_select(out=k.ident[:], in_=k.ident[:], compare_op=ALU.not_equal, fill=1.0,
                                        base=0, pattern=[[-1, P]], channel_multiplier=1)
                nc.gpsimd.memset(k.ones[:], 1.0)
                nc.gpsimd.memset(mhalf[:], -0.5).then_inc(consts, 1)
                for b in range(B):
                    pool.wait_ge(node_ready, b + 1)
                    pool.dma_start(a["node_dram"][b * N:(b + 1) * N, :].rearrange("(t p) u -> p (t u)", p=P),
                                   node[:, b * TB:(b + 1) * TB], allow_slow_non_contiguous=True).then_inc(node_stored, 16)
                    pool.wait_ge(node_stored, 16 * (b + 1))
                    for t in range(b * TB, (b + 1) * TB):
                        pool.indirect_dma_start(
                            node2[:, t:t + 1], None, a["node_dram"][:, :],
                            bass.IndirectOffsetOnAxis(ap=node[:, t:t + 1], axis=0)).then_inc(node2_in, 16)
                    pool.wait_ge(node2_in, 16 * TB * (b + 1))
                    if b >= 2:
                        pool.wait_ge(gT_done, b - 1)
                    for t in range(TB):
                        pool.indirect_dma_start(
                            gath[:, b % 2, t, :], None, a["ctx"][:, :],
                            bass.IndirectOffsetOnAxis(ap=node2[:, b * TB + t:b * TB + t + 1], axis=0)).then_inc(gath_in[b % 2], 16)
                for b in range(B):
                    for t in range(b * TB, (b + 1) * TB):
                        pool.wait_ge(z2_ready, t + 1)
                        nc.gpsimd.tensor_tensor(k.x[:, t, :], k.x[:, t, :], z2[:, t % 2, :], ALU.add).then_inc(x2_ready, 1)
                    if b == 1:
                        pool.wait_ge(var_ready, 1)
                        nc.gpsimd.tensor_tensor(rstd[:], rstd[:], mhalf[:], ALU.pow).then_inc(rstd_ready, 1)
                    if b == 2:
                        pool.wait_ge(bounds_ready, 1)
                        nc.gpsimd.partition_all_reduce(bounds_max[:, 0:3], bounds[:, 0:3], H, RMAX).then_inc(reduced, 1)
                        pool.wait_ge(rows_ready, 1)
                        nc.gpsimd.partition_all_reduce(rowstat_max[:], rowstat[:], P, RMAX).then_inc(reduced, 1)

            @block.tensor
            def _(pe):
                def first_layer(b):
                    pe.wait_ge(gath_in[b % 2], 16 * TB * (b // 2 + 1))
                    if b:
                        pe.wait_ge(gT_sb, b)
                    for t in range(TB):
                        last = nc.tensor.transpose(GT[:, t * P:(t + 1) * P], gath[:, b % 2, t, :], k.ident[:])
                    last.then_inc(gT_done, 1)
                    pe.wait_ge(gT_sb, b + 1)
                    for c in range(KC):
                        m = b * KC + c
                        if m >= 2:
                            pe.wait_ge(h1_ready, m - 1)
                        nc.tensor.matmul(L1[c % 2][:], w0[:, c * P:(c + 1) * P], gathT[:, b % 2, :],
                                         start=True, stop=True).then_inc(l1_done, 1)

                def second_layer(b):
                    for t in range(TB):
                        n = b * TB + t
                        if n >= 2:
                            pe.wait_ge(s2_ready, n - 1)
                        for c in range(KC):
                            if t == 0:
                                pe.wait_ge(h1_ready, b * KC + c + 1)
                            last = nc.tensor.matmul(L2[t % 2][:], h1T[:, b % 2, c, t * P:(t + 1) * P], w1[:, c, :],
                                                    start=(c == 0), stop=(c == KC - 1))
                        last.then_inc(l2_done, 1)

                pe.wait_ge(consts, 1)
                pe.wait_ge(w_in, 32)
                first_layer(0)
                pe.wait_ge(w1_in, 16 * (KC + 1))
                for b in range(B):
                    if b + 1 < B:
                        first_layer(b + 1)
                    second_layer(b)
                    if b == 0:
                        pe.wait_ge(absw_done, KC + 1)
                        nc.tensor.matmul(CS[0][:], k.ones[:], absw[:, KC, :], start=True, stop=True)
                        for c in range(KC):
                            last = nc.tensor.matmul(CS[1][:], k.ones[:], absw[:, c, :], start=(c == 0), stop=(c == KC - 1))
                        last.then_inc(colsum_done, 1)

            @block.scalar
            def _(act):
                def first_layer(b):
                    act.wait_ge(gT_done, b + 1)
                    if b >= 2:
                        act.wait_ge(l1_done, (b - 1) * KC)
                    nc.scalar.activation(gathT[:, b % 2, :], GT[:], ACT.Copy).then_inc(gT_sb, 1)
                    for c in range(KC):
                        m = b * KC + c
                        act.wait_ge(l1_done, m + 1)
                        if m >= 2:
                            act.wait_ge(l1_em, m - 1)
                        nc.scalar.activation(ex1[:, c % 2, :], L1[c % 2][:], ACT.Exp,
                                             bias=b0t[:, c:c + 1]).then_inc(l1_exp, 1)

                act.wait_ge(w_in, 32)
                nc.scalar.activation(absw[:, KC, :], w0[:], ACT.Abs).then_inc(absw_done, 1)
                act.wait_ge(w1_in, 16 * (KC + 1))
                for c in range(KC):
                    nc.scalar.activation(absw[:, c, :], w1[:, c, :], ACT.Abs).then_inc(absw_done, 1)
                first_layer(0)
                for b in range(B):
                    if b + 1 < B:
                        first_layer(b + 1)
                    for t in range(TB):
                        n = b * TB + t
                        act.wait_ge(s2_ready, n + 1)
                        if n >= 2:
                            act.wait_ge(em2_ready, n - 1)
                        nc.scalar.activation(ex2[:, t % 2, :], s2[:, t % 2, :], ACT.Exp).then_inc(l2_exp, 1)
                    if b == 0:
                        act.wait_ge(small_in, 80)
                        for j in range(4):
                            nc.scalar.activation(small[:, j, :], small[:, j, :], ACT.Abs,
                                                 accum_out=bounds[:, 3 + j:4 + j]).then_inc(abs_small, 1)
                        nc.scalar.activation(small[:, 4, :], small[:, 4, :], ACT.Abs).then_inc(abs_small, 1)
                        act.wait_ge(ctx_in, 16)
                        nc.scalar.activation(ctx_all[:], ctx_all[:], ACT.Abs).then_inc(abs_small, 1)

            @block.vector
            def _(dve):
                chain = [0]

                def link(ins):
                    chain[0] += 1
                    ins.then_inc(vch, 1)
                    dve.wait_ge(vch, chain[0])

                def first_layer(b):
                    for c in range(KC):
                        m = b * KC + c
                        dve.wait_ge(l1_exp, m + 1)
                        if m >= 2:
                            dve.wait_ge(h1_ready, m - 1)
                        nc.vector.tensor_scalar(em1[:, c % 2, :], ex1[:, c % 2, :], 1.0, -1.0,
                                                ALU.min, ALU.add).then_inc(l1_em, 1)
                        dve.wait_ge(l1_em, m + 1)
                        if b >= 2 and c == 0:
                            dve.wait_ge(l2_done, (b - 1) * TB)
                        nc.vector.scalar_tensor_tensor(h1T[:, b % 2, c, :], L1[c % 2][:], b0t[:, c:c + 1],
                                                       em1[:, c % 2, :], ALU.add, ALU.max).then_inc(h1_ready, 1)

                def elu2(n):
                    t = n % 2
                    dve.wait_ge(l2_exp, n + 1)
                    nc.vector.tensor_scalar(em2[:, t, :], ex2[:, t, :], 1.0, -1.0, ALU.min, ALU.add).then_inc(em2_ready, 1)
                    dve.wait_ge(em2_ready, n + 1)
                    if n >= 2:
                        dve.wait_ge(x2_ready, n - 1)
                    nc.vector.tensor_tensor(z2[:, t, :], s2[:, t, :], em2[:, t, :], ALU.max).then_inc(z2_ready, 1)

                for b in range(B):
                    dve.wait_ge(x_in[b], 16)
                    for t in range(b * TB, (b + 1) * TB):
                        last = nc.vector.max(top[:, t, :], k.x[:, t, :])
                    link(last)
                    for t in range(b * TB, (b + 1) * TB):
                        last = nc.vector.max_index(top_ix[:, t, :], top[:, t, :], k.x[:, t, :])
                    link(last)
                    nc.vector.tensor_scalar(node[:, b * TB:(b + 1) * TB], top_ix[:, b * TB:(b + 1) * TB, 0],
                                            float(b * N), None, ALU.add).then_inc(node_ready, 1)
                first_layer(0)
                for b in range(B):
                    if b + 1 < B:
                        first_layer(b + 1)
                    for t in range(TB):
                        n = b * TB + t
                        if b < 2:
                            for j in (2 * n, 2 * n + 1):
                                nc.vector.bn_stats(bn[:, j, :], k.x[:, j, :]).then_inc(bn_ready, 1)
                        dve.wait_ge(l2_done, n + 1)
                        if n >= 2:
                            dve.wait_ge(z2_ready, n - 1)
                        nc.vector.tensor_tensor(s2[:, t % 2, :], L2[t % 2][:], b1bc[:], ALU.add).then_inc(s2_ready, 1)
                        if n:
                            elu2(n - 1)
                    if b == 1:
                        dve.wait_ge(bn_ready, NT)
                        for t in range(NT):
                            last = nc.vector.bn_aggr(mv[:, t, :], bn[:, t, :])
                        link(last)
                        nc.vector.tensor_scalar(rstd[:], mv[:, :, 1], EPS, None, ALU.add).then_inc(var_ready, 1)
                        dve.wait_ge(abs_small, 6)
                        nc.vector.tensor_reduce(rowstat[:, 0:1], ctx_all[:], AX_X, ALU.max)
                        nc.vector.tensor_tensor(bounds[:, 0:1], bounds[:, 3:4], bounds[:, 4:5], ALU.add)
                        nc.vector.tensor_tensor(bounds[:, 1:2], bounds[:, 5:6], bounds[:, 6:7], ALU.add)
                        nc.vector.tensor_reduce(bounds[:, 2:3], small[:, 4, :], AX_X, ALU.max).then_inc(bounds_ready, 1)
                        dve.wait_ge(colsum_done, 1)
                        nc.vector.tensor_reduce(colsum[:, 0:1], CS[0][:], AX_X, ALU.max)
                        nc.vector.tensor_reduce(colsum[:, 1:2], CS[1][:], AX_X, ALU.max)
                    if b == 2:
                        link(nc.vector.tensor_tensor(gap[:], top[:, :, 0], top[:, :, 1], ALU.subtract))
                        link(nc.vector.tensor_tensor(lead[:], top[:, :, 0], mv[:, :, 0], ALU.subtract))
                        dve.wait_ge(rstd_ready, 1)
                        link(nc.vector.tensor_tensor(gap[:], gap[:], rstd[:], ALU.mult))
                        link(nc.vector.tensor_tensor(lead[:], lead[:], rstd[:], ALU.mult))
                        link(nc.vector.scalar_tensor_tensor(lead[:], lead[:], -1.0, lead[:], ALU.mult, ALU.max))
                        link(nc.vector.tensor_scalar(lead[:], lead[:], 1.0, 6e-7, ALU.add, ALU.mult))
                        link(nc.vector.scalar_tensor_tensor(gap[:], gap[:], -0.99, lead[:], ALU.mult, ALU.add))
                        nc.vector.tensor_reduce(rowstat[:, 1:2], gap[:], AX_X, ALU.max).then_inc(rows_ready, 1)
                elu2(NT - 1)
                dve.wait_ge(reduced, 2)
                f = fin
                link(nc.vector.tensor_tensor(f[:, 0:1], rowstat_max[0:1, 0:1], colsum[0:1, 0:1], ALU.mult))
                link(nc.vector.tensor_tensor(f[:, 1:2], f[:, 0:1], bounds_max[0:1, 2:3], ALU.add))
                link(nc.vector.tensor_tensor(f[:, 1:2], f[:, 1:2], colsum[0:1, 1:2], ALU.mult))
                link(nc.vector.tensor_tensor(f[:, 0:1], f[:, 0:1], bounds_max[0:1, 0:1], ALU.mult))
                link(nc.vector.scalar_tensor_tensor(f[:, 1:2], f[:, 1:2], bounds_max[0:1, 1:2], f[:, 0:1],
                                                    ALU.mult, ALU.add))
                link(nc.vector.tensor_scalar(f[:, 1:2], f[:, 1:2], -2.1 / MASK_VAL, -120.0 / MASK_VAL, ALU.mult, ALU.add))
                link(nc.vector.tensor_tensor(f[:, 2:3], f[:, 1:2], rowstat_max[0:1, 1:2], ALU.add))
                link(nc.vector.tensor_scalar(f[:, 3:4], f[:, 2:3], 0.0, -1.0, ALU.is_lt, ALU.mult))
                link(nc.vector.tensor_scalar(k.flag[:], f[:, 3:4], 1.0, None, ALU.add))
                if FORCE_GENERAL:
                    link(nc.vector.memset(k.flag[:], 1))


def general_block(nc, k, a):
    with ExitStack() as ctx:
        def sb(name, shape, dt=F32):
            return ctx.enter_context(nc.sbuf_tensor(name, shape, dt))

        loaded = ctx.enter_context(nc.semaphore("g_loaded"))
        nodes_in = ctx.enter_context(nc.semaphore("g_nodes_in"))
        g_passed = ctx.enter_context(nc.semaphore("g_passed"))
        xg = sb("g_x", [P, TB, D])
        cg = sb("g_ctx", [P, TB, FIN])
        bn = sb("g_bn", [P, TB, 6])
        mv = sb("g_mv", [P, TB, 2])
        rstd = sb("g_rstd", [P, TB])
        mhalf = sb("g_mhalf", [P, TB])
        mask = sb("g_mask", [P, TB, N])
        inT = sb("g_inT", [P, KC, N])
        feat = sb("g_feat", [P, TB, H * O])
        work = sb("g_work", [P, TB, N])
        attn = sb("g_attn", [P, 2, TB, H])
        diag = sb("g_diag", [P, TB, P])
        e = sb("g_e", [P, TB, N])
        pT = sb("g_pT", [P, TB, N])
        nmax = sb("g_nmax", [P, TB])
        total = sb("g_total", [P, TB])
        o = sb("g_o", [P, TB, H * O])
        w0 = sb("g_w0", [P, 1, H * O])
        w1 = sb("g_w1", [P, KC, H * O])
        avec = sb("g_avec", [P, 6, H * O])
        bank = k.psum

        def stage(vector=None, scalar=None, tensor=None, gpsimd=None, sync=None):
            with nc.Block() as block:
                if vector:
                    block.vector(lambda dve: vector())
                if scalar:
                    block.scalar(lambda act: scalar())
                if tensor:
                    block.tensor(lambda pe: tensor())
                if gpsimd:
                    block.gpsimd(lambda pool: gpsimd())
                if sync:
                    block.sync(sync)

        def flat(ap):
            return ap.rearrange("p t n -> p (t n)")

        def load_weights(sp):
            sp.dma_start(w0[:, 0, :].rearrange("f (h o) -> f h o", h=H), a["W0"].rearrange("h f o -> f h o")).then_inc(loaded, 16)
            for c in range(KC):
                sp.dma_start(w1[:, c, :].rearrange("f (h o) -> f h o", h=H),
                             a["W1"][:, c * P:(c + 1) * P, :].rearrange("h f o -> f h o")).then_inc(loaded, 16)
            for j, name in enumerate(("a_self0", "a_neigh0", "b0", "a_self1", "a_neigh1", "b1")):
                sp.dma_start(avec[:, j, :], a[name].rearrange("h o -> (h o)").rearrange("(u d) -> u d", u=1)
                             .broadcast_to([P, H * O])).then_inc(loaded, 16)
            sp.wait_ge(loaded, 16 * (1 + KC + 6))
        for engine in (nc.vector, nc.scalar, nc.tensor, nc.gpsimd, nc.sync):
            engine.sem_inc(g_passed, 1)
        stage(sync=load_weights, gpsimd=lambda: nc.gpsimd.memset(mhalf[:], -0.5))

        def each(f, n=TB):
            def run():
                for t in range(n):
                    f(t)
            return run

        def layer(chunks, w, at):
            def products():
                for t in range(TB):
                    for c in range(chunks):
                        nc.tensor.matmul(bank[t][:], inT[:, c, t * P:(t + 1) * P], w[:, c, :],
                                         start=(c == 0), stop=(c == chunks - 1))
            stage(tensor=products)
            stage(scalar=each(lambda t: nc.scalar.activation(feat[:, t, :], bank[t][:], ACT.Copy)))
            for j in range(2):
                stage(vector=each(lambda t: nc.vector.tensor_tensor(work[:, t, :], feat[:, t, :], avec[:, at + j, :], ALU.mult)))
                stage(vector=each(lambda t: nc.vector.tensor_reduce(
                    attn[:, j, t, :], work[:, t, :].rearrange("p (h o) -> p h o", h=H), AX_X, ALU.add)))
            with nc.Fori(0, H) as h:
                stage(vector=each(lambda t: nc.vector.tensor_scalar(
                    diag[:, t, :], k.ident[:], attn[:, 1, t, bass.ds(h, 1)], None, ALU.mult)))
                stage(tensor=each(lambda t: nc.tensor.matmul(bank[5][:, t * P:(t + 1) * P], k.ones[:], diag[:, t, :],
                                                             start=True, stop=True)))
                stage(vector=each(lambda t: nc.vector.tensor_scalar(
                    e[:, t, :], bank[5][:], attn[:, 0, t, bass.ds(h, 1)], None, ALU.add)))
                stage(vector=lambda: nc.vector.scalar_tensor_tensor(flat(work[:]), flat(e[:]), LRELU, flat(e[:]), ALU.mult, ALU.max))
                stage(vector=lambda: nc.vector.tensor_tensor(flat(e[:]), flat(work[:]), flat(mask[:]), ALU.add))
                stage(vector=lambda: nc.vector.tensor_reduce(nmax[:], e[:], AX_X, ALU.max))
                stage(vector=each(lambda t: nc.vector.tensor_scalar(work[:, t, :], e[:, t, :], nmax[:, t:t + 1], None, ALU.subtract)))
                stage(scalar=each(lambda t: nc.scalar.activation(e[:, t, :], work[:, t, :], ACT.Exp, accum_out=total[:, t:t + 1])))
                stage(tensor=each(lambda q: nc.tensor.transpose(bank[q // TB][:, (q % TB) * P:(q % TB + 1) * P],
                                                                e[:, q // TB, (q % TB) * P:(q % TB + 1) * P], k.ident[:]), TB * TB),
                      vector=lambda: nc.vector.reciprocal(nmax[:], total[:]))
                stage(scalar=each(lambda t: nc.scalar.activation(pT[:, t, :], bank[t][:], ACT.Copy)))

                def attend():
                    for t in range(TB):
                        for c in range(TB):
                            nc.tensor.matmul(bank[t][:, 0:O], pT[:, t, c * P:(c + 1) * P], feat[:, c, bass.ds(h * O, O)],
                                             start=(c == 0), stop=(c == TB - 1))
                stage(tensor=attend)
                stage(vector=each(lambda t: nc.vector.tensor_scalar(
                    o[:, t, bass.ds(h * O, O)], bank[t][:, 0:O], nmax[:, t:t + 1], None, ALU.mult)))
            stage(vector=each(lambda t: nc.vector.tensor_tensor(o[:, t, :], o[:, t, :], avec[:, at + 2, :], ALU.add)))
            stage(scalar=lambda: nc.scalar.activation(flat(work[:]), flat(o[:]), ACT.Exp))
            stage(vector=lambda: nc.vector.tensor_scalar(flat(work[:]), flat(work[:]), 1.0, -1.0, ALU.min, ALU.add))
            stage(vector=lambda: nc.vector.tensor_tensor(flat(o[:]), flat(o[:]), flat(work[:]), ALU.max))

        with nc.Fori(0, B) as b:
            def load(sp):
                sp.dma_start(xg[:], a["x"][bass.ds(b, 1)].rearrange("u (t p) d -> p (u t) d", p=P)).then_inc(nodes_in, 16)
                sp.dma_start(cg[:], a["ctx"][bass.ds(b * N, N), :].rearrange("(t p) f -> p t f", p=P)).then_inc(nodes_in, 16)
                sp.wait_ge(nodes_in, (b + 1) * 32)
                sp.sem_inc(g_passed, 1)
            stage(sync=load)
            stage(vector=each(lambda t: nc.vector.bn_stats(bn[:, t, :], xg[:, t, :])),
                  tensor=each(lambda t: nc.tensor.transpose(bank[0][:, t * P:(t + 1) * P], cg[:, t, :], k.ident[:])))
            stage(vector=each(lambda t: nc.vector.bn_aggr(mv[:, t, :], bn[:, t, :])),
                  scalar=lambda: nc.scalar.activation(inT[:, 0, :], bank[0][:], ACT.Copy))
            stage(vector=lambda: nc.vector.tensor_scalar(rstd[:], mv[:, :, 1], EPS, None, ALU.add))
            stage(gpsimd=lambda: nc.gpsimd.tensor_tensor(rstd[:], rstd[:], mhalf[:], ALU.pow))
            stage(vector=each(lambda t: nc.vector.tensor_scalar(work[:, t, :], xg[:, t, :], mv[:, t, 0:1], rstd[:, t:t + 1],
                                                                ALU.subtract, ALU.mult)))
            stage(vector=lambda: nc.vector.tensor_scalar(flat(mask[:]), flat(work[:]), -1.0, 1.0, ALU.mult, ALU.add))
            stage(vector=lambda: nc.vector.tensor_scalar(flat(mask[:]), flat(mask[:]), MASK_VAL, None, ALU.mult))
            layer(1, w0, 0)
            stage(tensor=each(lambda q: nc.tensor.transpose(bank[q // TB][:, (q % TB) * P:(q % TB + 1) * P],
                                                            o[:, q % TB, (q // TB) * P:(q // TB + 1) * P], k.ident[:]), KC * TB))
            stage(scalar=each(lambda c: nc.scalar.activation(inT[:, c, :], bank[c][:], ACT.Copy), KC))
            layer(KC, w1, 3)
            stage(vector=lambda: nc.vector.tensor_tensor(k.x[:, bass.ds(b * TB, TB), :], xg[:], o[:], ALU.add))


def experts_block(nc, k, a):
    with ExitStack() as ctx:
        def sb(name, shape, dt=F32):
            return ctx.enter_context(nc.sbuf_tensor(name, shape, dt))

        def sem(name):
            return ctx.enter_context(nc.semaphore(name))

        bank = k.psum
        gate_raw = sb("gate_raw", [E, D])
        gateT = sb("gateT", [P, KC, E])
        upT = sb("upT", [P, KC, 2 * SI])
        downT = sb("downT", [P, SC, D])
        bn = sb("bn_c", [P, 2, TB, 6])
        mv = sb("mv_c", [P, 2, TB, 2])
        rstd = sb("rstd_c", [P, 2, TB])
        mhalf = sb("mhalf_c", [P, TB])
        rows = sb("rows", [P, 2, TB, ROW])
        xnT = sb("xnT", [P, KC, T])
        raw_all = xnT[:].rearrange("p c t -> p (c t)")
        raw = raw_all[:, 0:2 * SC * D].rearrange("p (s d) -> p s d", d=D)
        raw_down = raw_all[:, 2 * SC * D:2 * SC * D + KC * SI].rearrange("p (c s) -> p c s", s=SI)
        top = sb("top_c", [P, TB, 8])
        nmax = sb("nmax", [P, TB])
        lg = sb("lg", [P, TB, E])
        ex = sb("ex", [P, TB, E])
        esum = sb("esum", [P, TB])
        rsum = sb("rsum", [P, TB])
        key = sb("key", [P, TB, E])
        ktop = sb("ktop", [P, TB, 8])
        kix = sb("kix", [P, TB, 8], U32)
        kixf = sb("kixf", [P, TB, 8])
        krep = sb("krep", [P, TB, E])
        iota_e = sb("iota_e", [P, E])
        iota_ei = sb("iota_ei", [P, E], I32)
        left = sb("left", [P, NT * E])
        order_i = sb("order_i", [P, HALF], I32)
        order = sb("order", [P, HALF])
        val = sb("val", [P, HALF])
        cand = sb("cand", [P, CAP])
        both = sb("both", [E, 2 * CAP])
        slots = sb("slots", [E, CAP])
        late = sb("late", [E, CAP])
        table = sb("table", [P, E], U32)
        sg = sb("sg", [P, N])
        shid = sb("shid", [P, SC, N])
        gu_w = sb("gu_w", [P, U, KC, 2 * I])
        dn_w = sb("dn_w", [IH, U, 2, D])
        gx = sb("gx", [P, U, ROW])
        gxT = sb("gxT", [P, 2, KC, P])
        slot_w = sb("slot_w", [P, 2, 1])
        eg = sb("eg", [P, I])
        hid = sb("hid", [P, 2, IH])
        hidT = sb("hidT", [IH, 2, 2, P])
        y = sb("y", [P, 2, D])
        idx_g = sb("idx_g", [P, U, 1], U32)
        idx_s = sb("idx_s", [P, 2, 1], U32)

        raw_in, wT_done, wT_sb = sem("raw_in"), sem("wT_done"), sem("wT_sb")
        lg_ready = sem("lg_ready")
        rows_out = [sem(f"rows_out{j}") for j in range(2)]
        cc, vch = sem("cc"), sem("vch_c")
        pool_passed = sem("pool_passed")
        var_ready, rstd_ready, xn_ready, xT_done, xT_sb = (
            sem(s) for s in ("var_ready_c", "rstd_ready_c", "xn_ready", "xT_done", "xT_sb"))
        logits, nmax_ready, exp_done, rows_full, left_ready, leftT_done, val_ready = (
            sem(s) for s in ("logits", "nmax_ready", "exp_done", "rows_full", "left_ready", "leftT_done", "val_ready"))
        cand_ready, both_in, slots_ready, slotsT_done, table_ready = (
            sem(s) for s in ("cand_ready", "both_in", "slots_ready", "slotsT_done", "table_ready"))
        sup_done, sg_ready, shid_ready, sdn_done, x3_ready, x3_out = (
            sem(s) for s in ("sup_done", "sg_ready", "shid_ready", "sdn_done", "x3_ready", "x3_out"))
        w_in = [sem(f"ew_in{u}") for u in range(U)]
        g_in = [sem(f"eg_in{u}") for u in range(U)]
        pidx, gT_done, gxT_ready, w_copied, gu_done, eg_ready, hid_ready, hT_done, hidT_ready, dn_done, y_ready, y_free, scat = (
            sem(s) for s in ("pidx", "egT_done", "gxT_ready", "w_copied", "gu_done", "eg_ready", "hid_ready",
                             "hT_done", "hidT_ready", "dn_done", "y_ready", "y_free", "scat"))

        wt = []
        for c in range(KC):
            wt.append(([gate_raw[:, :].rearrange("e (p c) -> e c p", c=KC)[:, c, :]], E, gateT[:, c, :]))
        for c in range(KC):
            for g in range(2):
                wt.append(([raw[:, g * SC + s, :].rearrange("q (p c) -> q c p", c=KC)[:, c, :] for s in range(SC)],
                           P, upT[:, c, g * SI:(g + 1) * SI]))
        for s in range(SC):
            wt.append(([raw_down[:, c, s * P:(s + 1) * P] for c in range(KC)], P, downT[:, s, :]))
        WB = 2
        XT, LG, UP, SD = bank[0:2], bank[2:4], bank[4:6], bank[6:8]

        with nc.Block() as block:
            def load_expert(sp, e, u):
                def of(name):
                    w = a[name]
                    return w[e] if isinstance(e, int) else w[bass.ds(e, 1)].rearrange("u r n -> (u r) n")
                sp.dma_start(gu_w[:, u, :, :], of("gate_up").rearrange("(p c) n -> p c n", c=KC)).then_inc(w_in[u], 16)
                sp.dma_start(dn_w[:, u, :, :], of("down").rearrange("(p j) n -> p j n", j=2)).then_inc(w_in[u], 16)

            @block.sync
            def _(sp):
                sp.dma_start(gate_raw[:], a["gate_w"]).then_inc(raw_in, 16)
                sp.dma_start(raw[:, 0:SC, :], a["sh_gate"].rearrange("(s p) d -> p s d", p=P)).then_inc(raw_in, 16)
                sp.dma_start(raw[:, SC:2 * SC, :], a["sh_up"].rearrange("(s p) d -> p s d", p=P)).then_inc(raw_in, 16)
                sp.dma_start(raw_down, a["sh_down"].rearrange("(c p) s -> p c s", p=P)).then_inc(raw_in, 16)
                for u in range(U):
                    load_expert(sp, u, u)
                for b in range(B):
                    sp.wait_ge(rows_full, b + 1)
                    sp.dma_start(a["rows_dram"][b * N:(b + 1) * N, :].rearrange("(t p) r -> p t r", p=P),
                                 rows[:, b % 2]).then_inc(rows_out[b % 2], 16)
                sp.wait_ge(cand_ready, 1)
                sp.dma_start(both[:, 0:CAP], cand[0:E, :]).then_inc(both_in, 16)
                sp.dma_start(both[:, CAP:2 * CAP], cand[E:2 * E, :]).then_inc(both_in, 16)
                for b in range(B):
                    sp.wait_ge(x3_ready, (b + 1) * TB)
                    sp.dma_start(a["out"][b * N:(b + 1) * N, :].rearrange("(t p) d -> p t d", p=P),
                                 k.x[:, b * TB:(b + 1) * TB, :]).then_inc(x3_out, 16)
                with sp.Fori(1, E // U) as i:
                    for u in range(U):
                        sp.wait_ge(dn_done, (i - 1) * U + u + 1)
                        load_expert(sp, i * U + u, u)

            @block.gpsimd
            def _(pool):
                nc.gpsimd.memset(mhalf[:], -0.5)
                nc.gpsimd.iota(iota_ei[:], pattern=[[1, E]], base=0, channel_multiplier=0).then_inc(cc, 1)
                for u in range(2):
                    pool.wait_ge(cc, u + 1)
                    nc.gpsimd.iota(order_i[u * E:(u + 1) * E, :], pattern=[[-2 * P, NT // 2], [-1, P]],
                                   base=3 * T - u * P, channel_multiplier=0).then_inc(cc, 1)
                pool.wait_ge(cc, 3)
                nc.gpsimd.tensor_copy(iota_e[:], iota_ei[:])
                nc.gpsimd.tensor_copy(order[:], order_i[:]).then_inc(cc, 1)
                for b in range(B):
                    pool.wait_ge(var_ready, b + 1)
                    nc.gpsimd.tensor_tensor(rstd[:, b % 2], rstd[:, b % 2], mhalf[:], ALU.pow).then_inc(rstd_ready, 1)

                def scatter(e, u):
                    if not (isinstance(e, int) and e == 0):
                        if due(e * 16):
                            pool.wait_ge(scat, e * 16)
                        pool.sem_inc(pool_passed, 1)
                    nc.gpsimd.tensor_copy(idx_s[:, u % 2, :], table[:, bass.ds(e, 1)]).then_inc(y_free, 1)
                    pool.wait_ge(y_free, e + 1)
                    pool.wait_ge(y_ready, e + 1)
                    pool.sem_inc(pool_passed, 1)
                    pool.indirect_dma_start(a["out"][:, :], bass.IndirectOffsetOnAxis(ap=idx_s[:, u % 2, :], axis=0),
                                            y[:, u % 2, :], None, compute_op=ALU.add).then_inc(scat, 16)

                pool.wait_ge(table_ready, 1)
                for j in range(2):
                    pool.wait_ge(rows_out[j], 16 * B // 2)
                for e in range(U - 1):
                    nc.gpsimd.tensor_copy(idx_g[:, e, :], table[:, e:e + 1]).then_inc(pidx, 1)
                    pool.wait_ge(pidx, e + 1)
                    pool.indirect_dma_start(gx[:, e, :], None, a["rows_dram"][:, :],
                                            bass.IndirectOffsetOnAxis(ap=idx_g[:, e, :], axis=0)).then_inc(g_in[e], 16)

                def gather_ahead(n, i, u):
                    e, s = n + U - 1, (u + U - 1) % U
                    if not (isinstance(n, int) and n == 0):
                        if due(n):
                            pool.wait_ge(gT_done, n)
                        if due(n):
                            pool.wait_ge(w_copied, n)
                        pool.sem_inc(pool_passed, 1)
                    nc.gpsimd.tensor_copy(idx_g[:, s, :], table[:, bass.ds(e, 1)]).then_inc(pidx, 1)
                    pool.wait_ge(pidx, n + U)
                    pool.sem_inc(pool_passed, 1)
                    pool.indirect_dma_start(gx[:, s, :], None, a["rows_dram"][:, :],
                                            bass.IndirectOffsetOnAxis(ap=idx_g[:, s, :], axis=0)).then_inc(g_in[s], 16)

                def turn(i, last):
                    for u in range(U):
                        n = i * U + u
                        if not (last and u > 0):
                            gather_ahead(n, i, u)
                        scatter(n, u)
                pool.wait_ge(x3_out, 16 * B)
                for i in turns(pool, E // U - 1):
                    turn(i, False)
                turn(E // U - 1, True)
                pool.wait_ge(scat, 16 * E)

            @block.tensor
            def _(pe):
                pe.wait_ge(raw_in, 64)
                for j, (parts, r, dst) in enumerate(wt):
                    if j >= WB:
                        pe.wait_ge(wT_sb, j - WB + 1)
                    for q, src in enumerate(parts):
                        last = nc.tensor.transpose(bank[j % WB][:, q * r:(q + 1) * r], src, k.ident[0:r, 0:r])
                    last.then_inc(wT_done, 1)
                pe.wait_ge(wT_sb, len(wt))
                def gate(b):
                    for t in range(TB):
                        n = b * TB + t
                        pe.wait_ge(xn_ready, n + 1)
                        if n >= 2:
                            pe.wait_ge(xT_sb, n - 1)
                        for c in range(KC):
                            last = nc.tensor.transpose(XT[t % 2][:, c * P:(c + 1) * P], rows[:, b % 2, t, c * P:(c + 1) * P],
                                                       k.ident[:])
                        last.then_inc(xT_done, 1)
                    if b >= 2:
                        pe.wait_ge(lg_ready, b - 1)
                    for t in range(TB):
                        n = b * TB + t
                        pe.wait_ge(xT_sb, n + 1)
                        for c in range(KC):
                            last = nc.tensor.matmul(LG[b % 2][:, t * E:(t + 1) * E], xnT[:, c, n * P:(n + 1) * P],
                                                    gateT[:, c, :], start=(c == 0), stop=(c == KC - 1))
                    last.then_inc(logits, 1)

                def shared_up(b, s):
                    if b + s:
                        pe.wait_ge(sg_ready, b * SC + s)
                        pe.wait_ge(shid_ready, b * SC + s)
                    for g in range(2):
                        for c in range(KC):
                            last = nc.tensor.matmul(UP[g][:], upT[:, c, g * SI + s * P:g * SI + (s + 1) * P],
                                                    xnT[:, c, b * N:(b + 1) * N], start=(c == 0), stop=(c == KC - 1))
                        last.then_inc(sup_done, 1)

                def shared_down(b):
                    for t in range(TB):
                        n = b * TB + t
                        if n >= 2:
                            pe.wait_ge(x3_ready, n - 1)
                        for s in range(SC):
                            if t == 0:
                                pe.wait_ge(shid_ready, b * SC + s + 1)
                            last = nc.tensor.matmul(SD[t % 2][:], shid[:, s, t * P:(t + 1) * P], downT[:, s, :],
                                                    start=(s == 0), stop=(s == SC - 1))
                        last.then_inc(sdn_done, 1)

                def shared(b):
                    for s in range(SC):
                        shared_up(b, s)
                        if b == 2 and s == 0:
                            pe.wait_ge(left_ready, B)
                            for j in range(NT // 2):
                                last = nc.tensor.transpose(bank[j // 4][:, (j % 4) * P:(j % 4 + 1) * P],
                                                           left[:, j * 2 * E:(j + 1) * 2 * E], k.ident[:])
                                if j % 4 == 3:
                                    last.then_inc(leftT_done, 1)
                    shared_down(b)

                gate(0)
                shared(0)
                gate(1)
                gate(2)
                shared(1)
                gate(3)
                shared(2)
                shared(3)
                pe.wait_ge(slots_ready, 1)
                nc.tensor.transpose(bank[2][:, 0:E], slots[:], k.ident[0:E, 0:E]).then_inc(slotsT_done, 1)

                GT, GU, HT, DN = bank[0:2], bank[4:6], bank[3], bank[6]

                def transposes(n, u, i1):
                    pe.wait_ge(g_in[u % U], 16 * i1)
                    for c in range(KC):
                        last = nc.tensor.transpose(GT[u % 2][:, c * P:(c + 1) * P], gx[:, u % U, c * P:(c + 1) * P], k.ident[:])
                    last.then_inc(gT_done, 1)

                def down(n, u):
                    pe.wait_ge(hidT_ready, n + 1)
                    if due(n):
                        pe.wait_ge(y_ready, n)
                    for j in range(2):
                        last = nc.tensor.matmul(DN[:], hidT[:, u % 2, j, :], dn_w[:, u % U, j, :],
                                                start=(j == 0), stop=(j == 1))
                    last.then_inc(dn_done, 1)

                def step(i, u, first, last_step):
                    n = i * U + u
                    pe.wait_ge(w_in[u], (i + 1) * 32)
                    pe.wait_ge(gxT_ready, n + 1)
                    for c in range(KC):
                        last = nc.tensor.matmul(GU[u % 2][:, 0:2 * I], gxT[:, u % 2, c, :], gu_w[:, u, c, :],
                                                start=(c == 0), stop=(c == KC - 1))
                    last.then_inc(gu_done, 1)
                    if not last_step:
                        transposes(n + 1, u + 1, i + 1 + (u + 1) // U)
                    if not first:
                        down(n - 1, (u - 1) % U)
                    pe.wait_ge(hid_ready, n + 1)
                    for j in range(2):
                        last = nc.tensor.transpose(HT[0:IH, j * P:(j + 1) * P], hid[:, j, :], k.ident[:])
                    last.then_inc(hT_done, 1)

                pe.wait_ge(table_ready, 1)
                pe.wait_ge(x3_ready, NT)
                transposes(0, 0, 1)
                for u in range(U):
                    step(0, u, u == 0, False)
                with pe.Fori(1, E // U - 1) as i:
                    for u in range(U):
                        step(i, u, False, False)
                for u in range(U):
                    step(E // U - 1, u, False, u == U - 1)
                down(E - 1, U - 1)

            @block.scalar
            def _(act):
                for j, (parts, r, dst) in enumerate(wt):
                    act.wait_ge(wT_done, j + 1)
                    nc.scalar.activation(dst, bank[j % WB][:, 0:r * len(parts)], ACT.Copy).then_inc(wT_sb, 1)
                def transposed(b):
                    for t in range(TB):
                        n = b * TB + t
                        act.wait_ge(xT_done, n + 1)
                        nc.scalar.activation(xnT[:, :, n * P:(n + 1) * P], XT[t % 2][:].rearrange("p (c q) -> p c q", c=KC),
                                             ACT.Copy).then_inc(xT_sb, 1)

                def gate_exp(b):
                    act.wait_ge(nmax_ready, b + 1)
                    if b:
                        act.wait_ge(rows_full, b)
                    for t in range(TB):
                        last = nc.scalar.activation(ex[:, t, :], lg[:, t, :], ACT.Exp, bias=nmax[:, t:t + 1],
                                                    accum_out=esum[:, t:t + 1])
                    last.then_inc(exp_done, 1)

                def silu(b):
                    for s in range(SC):
                        act.wait_ge(sup_done, b * (2 * SC) + 2 * s + 1)
                        if b + s:
                            act.wait_ge(shid_ready, b * SC + s)
                        nc.scalar.activation(sg[:], UP[0][:], ACT.Silu).then_inc(sg_ready, 1)

                transposed(0)
                gate_exp(0)
                silu(0)
                transposed(1)
                transposed(2)
                gate_exp(1)
                gate_exp(2)
                silu(1)
                transposed(3)
                gate_exp(3)
                silu(2)
                silu(3)

                def gx_copy(n, u):
                    act.wait_ge(gT_done, n + 1)
                    nc.scalar.activation(gxT[:, u % 2, :, :].rearrange("p c q -> p (c q)"), bank[u % 2][:],
                                         ACT.Copy).then_inc(gxT_ready, 1)

                def step(i, u, last_step):
                    n = i * U + u
                    act.wait_ge(gu_done, n + 1)
                    if due(n):
                        act.wait_ge(hid_ready, n)
                    nc.scalar.activation(eg[:], bank[4 + u % 2][:, 0:I], ACT.Silu).then_inc(eg_ready, 1)
                    if not last_step:
                        gx_copy(n + 1, u + 1)
                gx_copy(0, 0)
                for i in turns(act, E // U - 1):
                    for u in range(U):
                        step(i, u, False)
                for u in range(U):
                    step(E // U - 1, u, u == U - 1)

            @block.vector
            def _(dve):
                dve.wait_ge(cc, 4)
                chain = [0]

                def link(ins):
                    chain[0] += 1
                    ins.then_inc(vch, 1)
                    dve.wait_ge(vch, chain[0])

                def moments(b):
                    for t in range(TB):
                        last = nc.vector.bn_stats(bn[:, b % 2, t, :], k.x[:, b * TB + t, :])
                    link(last)
                    for t in range(TB):
                        last = nc.vector.bn_aggr(mv[:, b % 2, t, :], bn[:, b % 2, t, :])
                    link(last)
                    nc.vector.tensor_scalar(rstd[:, b % 2], mv[:, b % 2, :, 1], EPS, None, ALU.add).then_inc(var_ready, 1)

                def norm(b):
                    dve.wait_ge(rstd_ready, b + 1)
                    if b >= 2:
                        dve.wait_ge(rows_out[b % 2], 16)
                        dve.wait_ge(xT_done, (b - 1) * TB)
                    for t in range(TB):
                        nc.vector.tensor_scalar(
                            rows[:, b % 2, t, 0:D].rearrange("q (c p) -> q c p", c=KC),
                            k.x[:, b * TB + t, :].rearrange("q (p c) -> q c p", c=KC),
                            mv[:, b % 2, t, 0:1], rstd[:, b % 2, t:t + 1], ALU.subtract, ALU.mult).then_inc(xn_ready, 1)

                def route(b):
                    dve.wait_ge(logits, b + 1)
                    if b:
                        dve.wait_ge(exp_done, b)
                    nc.vector.tensor_copy(lg[:].rearrange("p t e -> p (t e)"), LG[b % 2][:, 0:TB * E]).then_inc(lg_ready, 1)
                    dve.wait_ge(lg_ready, b + 1)
                    for t in range(TB):
                        last = nc.vector.max(top[:, t, :], lg[:, t, :])
                    link(last)
                    nc.vector.tensor_scalar(nmax[:], top[:, :, 0], -1.0, None, ALU.mult).then_inc(nmax_ready, 1)
                    for t in range(TB):
                        last = nc.vector.tensor_scalar(key[:, t, :], lg[:, t, :], top[:, t, 0:1], EXP_FLOOR,
                                                       ALU.subtract, ALU.max)
                    link(last)
                    for t in range(TB):
                        last = nc.vector.max(ktop[:, t, :], key[:, t, :])
                    link(last)
                    for t in range(TB):
                        nc.vector.match_replace(krep[:, t, :], ktop[:, t, :], key[:, t, :], -1000.0)
                        last = nc.vector.max_index(kix[:, t, :], ktop[:, t, :], key[:, t, :])
                    link(last)
                    nc.vector.tensor_copy(kixf[:], kix[:])
                    link(nc.vector.tensor_scalar(krep[:], krep[:], -500.0, None, ALU.is_gt))
                    for j in (TOPK, TOPK + 1):
                        for t in range(TB):
                            last = nc.vector.scalar_tensor_tensor(krep[:, t, :], iota_e[:], kixf[:, t, j:j + 1],
                                                                  krep[:, t, :], ALU.is_equal, ALU.add)
                        link(last)
                    nc.vector.tensor_copy(left[:, b * TB * E:(b + 1) * TB * E],
                                          krep[:].rearrange("p t e -> p (t e)")).then_inc(left_ready, 1)
                    dve.wait_ge(exp_done, b + 1)
                    nc.vector.reciprocal(rsum[:], esum[:])
                    link(nc.vector.scalar_tensor_tensor(ex[:], krep[:], 0.0, ex[:], ALU.is_equal, ALU.mult))
                    for t in range(TB):
                        last = nc.vector.tensor_scalar(rows[:, b % 2, t, D:ROW], ex[:, t, :], rsum[:, t:t + 1], None, ALU.mult)
                    last.then_inc(rows_full, 1)
                    dve.wait_ge(rows_full, b + 1)

                def shared_up(b, s):
                    dve.wait_ge(sup_done, b * (2 * SC) + 2 * s + 2)
                    dve.wait_ge(sg_ready, b * SC + s + 1)
                    if s == 0 and b:
                        dve.wait_ge(sdn_done, b * TB)
                    nc.vector.tensor_tensor(shid[:, s, :], UP[1][:], sg[:], ALU.mult).then_inc(shid_ready, 1)

                def shared_down(b, t):
                    n = b * TB + t
                    dve.wait_ge(sdn_done, n + 1)
                    nc.vector.tensor_tensor(k.x[:, n, :], SD[t % 2][:], k.x[:, n, :], ALU.add).then_inc(x3_ready, 1)

                def extract(r):
                    link(nc.vector.max(cand[:, r * 8:(r + 1) * 8], val[:]))
                    last = nc.vector.match_replace(val[:], cand[:, r * 8:(r + 1) * 8], val[:], 0.0)
                    if r == R - 1:
                        last.then_inc(cand_ready, 1)
                    else:
                        link(last)

                def merge(r):
                    link(nc.vector.max(slots[:, r * 8:(r + 1) * 8], both[:]))
                    if r < R - 1:
                        link(nc.vector.match_replace(both[:], slots[:, r * 8:(r + 1) * 8], both[:], 0.0))

                R = CAP // 8
                moments(0)
                moments(1)
                norm(0)
                norm(1)
                route(0)
                moments(2)
                shared_up(0, 0)
                norm(2)
                moments(3)
                shared_up(0, 1)
                shared_up(0, 2)
                for t in range(TB):
                    shared_down(0, t)
                route(1)
                norm(3)
                route(2)
                for s in range(SC):
                    shared_up(1, s)
                for t in range(TB):
                    shared_down(1, t)
                route(3)
                shared_up(2, 0)
                for q in range(2):
                    dve.wait_ge(leftT_done, q + 1)
                    link(nc.vector.scalar_tensor_tensor(val[:, q * 512:(q + 1) * 512], bank[q][:], -2.0 * T,
                                                        order[:, q * 512:(q + 1) * 512], ALU.mult, ALU.add))
                rounds = iter(range(R))
                for _ in range(2):
                    extract(next(rounds))
                shared_up(2, 1)
                for _ in range(2):
                    extract(next(rounds))
                shared_up(2, 2)
                for t in range(TB):
                    extract(next(rounds))
                    shared_down(2, t)
                for s in range(2):
                    for _ in range(3):
                        extract(next(rounds))
                    shared_up(3, s)
                for r in rounds:
                    extract(r)
                shared_up(3, 2)
                dve.wait_ge(both_in, 32)
                for r in range(0, R):
                    merge(r)
                    if r % 4 == 3:
                        shared_down(3, r // 4)
                link(nc.vector.tensor_scalar(late[:], slots[:], float(T) + 0.5, 2.0 * T, ALU.is_gt, ALU.mult))
                link(nc.vector.scalar_tensor_tensor(late[:], late[:], float(T), slots[:], ALU.add, ALU.subtract))
                nc.vector.tensor_copy(slots[:], late[:]).then_inc(slots_ready, 1)
                dve.wait_ge(slotsT_done, 1)
                nc.vector.tensor_copy(table[:], bank[2][:, 0:E]).then_inc(table_ready, 1)

                def scaled(n, u):
                    dve.wait_ge(dn_done, n + 1)
                    dve.wait_ge(y_free, n + 1)
                    nc.vector.tensor_scalar(y[:, u % 2, :], bank[6][:], slot_w[:, u % 2, :], None, ALU.mult).then_inc(y_ready, 1)

                def step(i, u, first):
                    n = i * U + u
                    dve.wait_ge(gT_done, n + 1)
                    if not (isinstance(n, int) and n < 2):
                        if due(n - 1):
                            dve.wait_ge(y_ready, n - 1)
                    nc.vector.tensor_copy(slot_w[:, u % 2, :], gx[:, u, bass.ds(n + D, 1)]).then_inc(w_copied, 1)
                    dve.wait_ge(eg_ready, n + 1)
                    if due(n):
                        dve.wait_ge(hT_done, n)
                    nc.vector.tensor_tensor(hid[:].rearrange("s j p -> s p j"), bank[4 + u % 2][:, I:2 * I].rearrange("s (p j) -> s p j", j=2),
                                            eg[:].rearrange("s (p j) -> s p j", j=2), ALU.mult).then_inc(hid_ready, 1)
                    if not first:
                        scaled(n - 1, (u - 1) % U)
                    dve.wait_ge(hT_done, n + 1)
                    nc.vector.tensor_copy(hidT[:, u % 2, :, :].rearrange("p j q -> p (j q)"), bank[3][0:IH, 0:2 * P]).then_inc(hidT_ready, 1)
                for u in range(U):
                    step(0, u, u == 0)
                with dve.Fori(1, E // U) as i:
                    for u in range(U):
                        step(i, u, False)
                scaled(E - 1, U - 1)


def build(nc, a):
    k = Kernel()
    with ExitStack() as ctx:
        allocate(nc, ctx, k)
        attention_block(nc, k, a)
        flag = nc.values_load(k.flag[0:1, 0:1], min_val=0, max_val=1)
        with nc.If(flag > 0):
            general_block(nc, k, a)
        nc.end_ifs()
        experts_block(nc, k, a)


_INS = {"x": "x", "ctx_512": "ctx", "L0_xattn_W0": "W0", "L0_xattn_a_self0": "a_self0",
        "L0_xattn_a_neigh0": "a_neigh0", "L0_xattn_b0": "b0", "L0_xattn_W1": "W1",
        "L0_xattn_a_self1": "a_self1", "L0_xattn_a_neigh1": "a_neigh1", "L0_xattn_b1": "b1",
        "L0_ffn_gate_w": "gate_w", "L0_ffn_gate_up_proj": "gate_up", "L0_ffn_down_proj": "down",
        "L0_ffn_shared_gate_w": "sh_gate", "L0_ffn_shared_up_w": "sh_up", "L0_ffn_shared_down_w": "sh_down"}


def kernel(**inputs):
    import numpy as _np
    import concourse.bacc as _bacc
    from concourse.bass_utils import run_bass_kernel_spmd as _run

    nc = _bacc.Bacc("TRN2", target_bir_lowering=False, num_devices=1)
    arrays, a = {}, {}
    for name, short in _INS.items():
        v = _np.ascontiguousarray(inputs[name])
        if short == "ctx":
            v = v.reshape(T, FIN)
        arrays[f"in_{short}"] = v
        a[short] = nc.dram_tensor(f"in_{short}", v.shape, mybir.dt.from_np(v.dtype), kind="ExternalInput").ap()
    a["out"] = nc.dram_tensor("out", (T, D), F32, kind="ExternalOutput").ap()
    a["node_dram"] = nc.dram_tensor("node_dram", (T, 1), U32, kind="Internal").ap()
    a["rows_dram"] = nc.dram_tensor("rows_dram", (T, ROW), F32, kind="Internal").ap()
    build(nc, a)
    r = _run(nc, [arrays], core_ids=[0])
    return r.results[0]["out"].reshape(B, N, D)
```

```python
from contextlib import ExitStack

import concourse.bass as bass
import concourse.mybir as mybir

F32 = mybir.dt.float32
U32 = mybir.dt.uint32
I32 = mybir.dt.int32
ALU = mybir.AluOpType
ACT = mybir.ActivationFunctionType
AX_X = mybir.AxisListType.X
RMAX = bass.bass_isa.ReduceOp.max

P = 128
B, N, D = 4, 512, 512
FIN, H, O = 128, 8, 64
T = B * N
NT = T // P
TB = N // P
KC = D // P
E, TOPK, CAP = 64, 6, 128
I = 192
IH = I // 2
SI = 2 * I
SC = SI // P
ROW = D + E
EPS = 1e-5
LRELU = 0.2
MASK_VAL = -1e10
U = 4
EXP_FLOOR = -87.336
HALF = T // 2


def due(value):
    return not (isinstance(value, int) and value <= 0)


def turns(engine, n):
    yield 0
    with engine.Fori(1, n) as i:
        yield i




class Kernel:
    pass


def allocate(nc, ctx, k):
    def sb(name, shape, dt=F32):
        return ctx.enter_context(nc.sbuf_tensor(name, shape, dt))

    k.x = sb("x", [P, NT, D])
    k.ident = sb("ident", [P, P])
    k.ones = sb("ones", [P, P])
    k.flag = sb("flag", [1, 1], I32)
    k.gateT = sb("gateT", [P, KC, E])
    k.upT = sb("upT", [P, KC, 2 * SI])
    k.downT = sb("downT", [P, SC, D])
    k.mhalf = sb("mhalf", [P, NT])
    k.mv = sb("mv", [P, NT, 2])
    k.rstd = sb("rstd", [P, NT])
    k.iota_e = sb("iota_e", [P, E])
    k.order = sb("order", [P, HALF])
    k.psum = [ctx.enter_context(nc.psum_tensor(f"bank{i}", [P, 512], F32)) for i in range(8)]


def attention_block(nc, k, a):
    with ExitStack() as ctx:
        def sb(name, shape, dt=F32):
            return ctx.enter_context(nc.sbuf_tensor(name, shape, dt))

        def sem(name):
            return ctx.enter_context(nc.semaphore(name))

        w0 = sb("w0", [P, H * O])
        w1 = sb("w1", [P, KC, H * O])
        absw = sb("absw", [P, KC + 1, H * O])
        b0t = sb("b0t", [P, KC])
        b1bc = sb("b1bc", [P, H * O])
        nodes = sb("nodes", [P, NT, FIN])
        small = sb("small", [H, 5, O])
        bounds = sb("bounds", [H, 8])
        bounds_max = sb("bounds_max", [H, 4])
        rowstat = sb("rowstat", [P, 2])
        rowstat_max = sb("rowstat_max", [P, 2])
        colsum = sb("colsum", [P, 2])
        fin = sb("fin", [1, 8])
        top = sb("top", [P, NT, 8])
        top_ix = sb("top_ix", [P, NT, 8], U32)
        node = sb("node", [P, NT], U32)
        node2 = sb("node2", [P, NT], U32)
        bn = sb("bn", [P, NT, 6])
        bn2 = sb("bn2", [P, NT, 6])
        mv = sb("mv_x", [P, NT, 2])
        rstd = sb("rstd_x", [P, NT])
        gap = sb("gap", [P, NT])
        lead = sb("lead", [P, NT])
        ctxT = sb("ctxT", [P, 2, N])
        h1T = sb("h1T", [P, 2, KC, N])
        ex1 = sb("ex1", [P, 2, N])
        re1 = sb("re1", [P, 2, N])
        s2 = sb("s2", [P, 2, H * O])
        ex2 = sb("ex2", [P, 2, H * O])
        re2 = sb("re2", [P, 2, H * O])
        feat = sb("feat", [P, 2, TB, H * O])
        picked = sb("picked", [P, 2, TB, H * O])
        iota_ei = sb("iota_ei", [P, E], I32)
        order_i = sb("order_i", [P, HALF], I32)
        gate_raw = sb("gate_raw", [E, D])
        raw = sb("raw", [P, 2 * SC, D])
        raw_down = sb("raw_down", [P, KC, SI])

        x_in = [sem(f"x_in{b}") for b in range(B)]
        nodes_in = [sem(f"nodes_in{b}") for b in range(B)]
        w_in, small_in, w1_in = sem("w_in"), sem("small_in"), sem("w1_in")
        consts = sem("consts")
        vch = sem("vch")
        node_ready = sem("node_ready")
        node2_in = [sem(f"node2_in{j}") for j in range(2)]
        node_stored = [sem(f"node_stored{j}") for j in range(2)]
        feat_out = [sem(f"feat_out{j}") for j in range(2)]
        picked_in = [[sem(f"picked_in{j}_{t}") for t in range(TB)] for j in range(2)]
        gT_done, gT_sb = sem("gT_done"), sem("gT_sb")
        l1_done, l1_exp, h1_ready = (sem(s) for s in ("l1_done", "l1_exp", "h1_ready"))
        l2_done, s2_ready, l2_exp, z2_ready, x2_ready = (sem(s) for s in ("l2_done", "s2_ready", "l2_exp", "z2_ready", "x2_ready"))
        absw_done, colsum_done, abs_small, bounds_ready, reduced, rstd_ready, var_ready, rows_ready = (
            sem(s) for s in ("absw_done", "colsum_done", "abs_small", "bounds_ready", "reduced", "rstd_ready", "var_ready", "rows_ready"))
        var2_ready = sem("var2_ready")
        pch, bn_ready, top_ready, ix_ready = (sem(s) for s in ("pch", "bn_ready", "top_ready", "ix_ready"))
        raw_in, wT_done, wT_sb = sem("raw_in"), sem("wT_done"), sem("wT_sb")

        bank = k.psum
        GT, L1, L2 = bank[0], bank[1:3], bank[3:5]
        CS = bank[5:7]
        WT = bank[1:3]

        wt = []
        for c in range(KC):
            wt.append(([gate_raw[:, :].rearrange("e (p c) -> e c p", c=KC)[:, c, :]], E, k.gateT[:, c, :]))
        for c in range(KC):
            for g in range(2):
                wt.append(([raw[:, g * SC + s, :].rearrange("q (p c) -> q c p", c=KC)[:, c, :] for s in range(SC)],
                           P, k.upT[:, c, g * SI:(g + 1) * SI]))
        for s in range(SC):
            wt.append(([raw_down[:, c, s * P:(s + 1) * P] for c in range(KC)], P, k.downT[:, s, :]))

        with nc.Block() as block:
            @block.sync
            def _(sp):
                def load_nodes(b):
                    sp.dma_start(nodes[:, b * TB:(b + 1) * TB, :],
                                 a["ctx"][b * N:(b + 1) * N, :].rearrange("(t p) f -> p t f", p=P)).then_inc(nodes_in[b], 16)

                def load_x(b):
                    sp.dma_start(k.x[:, b * TB:(b + 1) * TB, :],
                                 a["x"][b].rearrange("(t p) d -> p t d", p=P)).then_inc(x_in[b], 16)

                load_nodes(0)
                sp.dma_start(w0[:].rearrange("f (h o) -> f h o", h=H),
                             a["W0"].rearrange("h f o -> f h o")).then_inc(w_in, 16)
                sp.dma_start(b0t[:], a["b0"].rearrange("h o -> (h o)").rearrange("(c p) -> p c", p=P),
                             allow_slow_non_contiguous=True).then_inc(w_in, 16)
                load_nodes(1)
                load_x(0)
                for c in range(KC):
                    sp.dma_start(w1[:, c, :].rearrange("f (h o) -> f h o", h=H),
                                 a["W1"][:, c * P:(c + 1) * P, :].rearrange("h f o -> f h o")).then_inc(w1_in, 16)
                sp.dma_start(b1bc[:], a["b1"].rearrange("h o -> (h o)").rearrange("(u d) -> u d", u=1)
                             .broadcast_to([P, H * O])).then_inc(w1_in, 16)
                load_x(1)
                load_nodes(2)
                load_x(2)
                load_x(3)
                load_nodes(3)
                for j, name in enumerate(("a_self0", "a_neigh0", "a_self1", "a_neigh1", "b0")):
                    sp.dma_start(small[:, j, :], a[name]).then_inc(small_in, 16)
                sp.dma_start(gate_raw[:], a["gate_w"]).then_inc(raw_in, 16)
                sp.dma_start(raw[:, 0:SC, :], a["sh_gate"].rearrange("(s p) d -> p s d", p=P)).then_inc(raw_in, 16)
                sp.dma_start(raw[:, SC:2 * SC, :], a["sh_up"].rearrange("(s p) d -> p s d", p=P)).then_inc(raw_in, 16)
                sp.dma_start(raw_down[:], a["sh_down"].rearrange("(c p) s -> p c s", p=P)).then_inc(raw_in, 16)
                for b in range(B):
                    sp.wait_ge(z2_ready, (b + 1) * TB)
                    sp.dma_start(a[f"feat_dram{b}"].rearrange("(t p) d -> p t d", p=P),
                                 feat[:, b % 2]).then_inc(feat_out[b % 2], 16)

            @block.gpsimd
            def _(pool):
                nc.gpsimd.memset(k.ident[:], 0.0).then_inc(pch, 1)
                pool.wait_ge(pch, 1)
                nc.gpsimd.affine_select(out=k.ident[:], in_=k.ident[:], compare_op=ALU.not_equal, fill=1.0,
                                        base=0, pattern=[[-1, P]], channel_multiplier=1)
                nc.gpsimd.memset(k.ones[:], 1.0)
                nc.gpsimd.memset(k.mhalf[:], -0.5).then_inc(consts, 1)
                nc.gpsimd.iota(iota_ei[:], pattern=[[1, E]], base=0, channel_multiplier=0).then_inc(pch, 1)
                for u in range(2):
                    pool.wait_ge(pch, u + 2)
                    nc.gpsimd.iota(order_i[u * E:(u + 1) * E, :], pattern=[[-2 * P, NT // 2], [-1, P]],
                                   base=3 * T - u * P, channel_multiplier=0).then_inc(pch, 1)
                pool.wait_ge(pch, 4)
                nc.gpsimd.tensor_copy(k.iota_e[:], iota_ei[:])
                nc.gpsimd.tensor_copy(k.order[:], order_i[:])

                def store_node(b):
                    pool.wait_ge(node_ready, b + 1)
                    pool.dma_start(a[f"node_dram{b}"].rearrange("(t p) u -> p (t u)", p=P),
                                   node[:, b * TB:(b + 1) * TB], allow_slow_non_contiguous=True).then_inc(node_stored[b % 2], 16)

                def node_of_node(b):
                    pool.wait_ge(node_stored[b % 2], 16 * (b // 2 + 1))
                    for t in range(b * TB, (b + 1) * TB):
                        pool.indirect_dma_start(
                            node2[:, t:t + 1], None, a[f"node_dram{b}"],
                            bass.IndirectOffsetOnAxis(ap=node[:, t:t + 1], axis=0)).then_inc(node2_in[b % 2], 16)

                def pick(b):
                    pool.wait_ge(node2_in[b % 2], 16 * TB * (b // 2 + 1))
                    pool.wait_ge(feat_out[b % 2], 16 * (b // 2 + 1))
                    if b >= 2:
                        pool.wait_ge(x2_ready, (b - 1) * TB)
                    for t in range(TB):
                        pool.indirect_dma_start(
                            picked[:, b % 2, t, :], None, a[f"feat_dram{b}"],
                            bass.IndirectOffsetOnAxis(ap=node2[:, b * TB + t:b * TB + t + 1], axis=0)).then_inc(picked_in[b % 2][t], 16)

                def add(b):
                    for t in range(TB):
                        n = b * TB + t
                        pool.wait_ge(picked_in[b % 2][t], 16 * (b // 2 + 1))
                        nc.gpsimd.tensor_tensor(k.x[:, n, :], k.x[:, n, :], picked[:, b % 2, t, :], ALU.add).then_inc(x2_ready, 1)

                store_node(0)
                node_of_node(0)
                store_node(1)
                node_of_node(1)
                pick(0)
                add(0)
                store_node(2)
                node_of_node(2)
                pick(1)
                store_node(3)
                add(1)
                node_of_node(3)
                pick(2)
                pool.wait_ge(var_ready, 1)
                nc.gpsimd.tensor_tensor(rstd[:], rstd[:], k.mhalf[:], ALU.pow).then_inc(rstd_ready, 1)
                pool.wait_ge(bounds_ready, 2)
                nc.gpsimd.partition_all_reduce(bounds_max[:, 0:3], bounds[:, 0:3], H, RMAX).then_inc(reduced, 1)
                nc.gpsimd.partition_all_reduce(rowstat_max[:, 0:1], rowstat[:, 0:1], P, RMAX).then_inc(reduced, 1)
                pick(3)
                pool.wait_ge(rows_ready, 1)
                nc.gpsimd.partition_all_reduce(rowstat_max[:, 1:2], rowstat[:, 1:2], P, RMAX).then_inc(reduced, 1)
                pool.wait_ge(var2_ready, B - 1)
                nc.gpsimd.tensor_tensor(k.rstd[:, 0:(B - 1) * TB], k.rstd[:, 0:(B - 1) * TB], k.mhalf[:, 0:(B - 1) * TB], ALU.pow)

            @block.tensor
            def _(pe):
                def transposes(b):
                    pe.wait_ge(nodes_in[b], 16)
                    if b:
                        pe.wait_ge(gT_sb, b)
                    for t in range(TB):
                        last = nc.tensor.transpose(GT[:, t * P:(t + 1) * P], nodes[:, b * TB + t, :], k.ident[:])
                    last.then_inc(gT_done, 1)

                def first_layer(b, c):
                    m = b * KC + c
                    if c == 0:
                        pe.wait_ge(gT_sb, b + 1)
                    if m >= 2:
                        pe.wait_ge(l1_exp, m - 1)
                    nc.tensor.matmul(L1[c % 2][:], w0[:, c * P:(c + 1) * P], ctxT[:, b % 2, :],
                                     start=True, stop=True).then_inc(l1_done, 1)

                def second_layer(b, t):
                    n = b * TB + t
                    if n >= 2:
                        pe.wait_ge(s2_ready, n - 1)
                    for c in range(KC):
                        if t == 0:
                            pe.wait_ge(h1_ready, b * KC + c + 1)
                        last = nc.tensor.matmul(L2[t % 2][:], h1T[:, b % 2, c, t * P:(t + 1) * P], w1[:, c, :],
                                                start=(c == 0), stop=(c == KC - 1))
                    last.then_inc(l2_done, 1)

                pe.wait_ge(consts, 1)
                pe.wait_ge(w_in, 32)
                transposes(0)
                for c in range(KC):
                    first_layer(0, c)
                transposes(1)
                pe.wait_ge(w1_in, 16 * (KC + 1))
                for b in range(B):
                    for t in range(TB):
                        if b + 1 < B:
                            first_layer(b + 1, t)
                        if b + 2 < B and t == TB - 1:
                            transposes(b + 2)
                        second_layer(b, t)
                    if b == 1:
                        pe.wait_ge(absw_done, KC + 1)
                        nc.tensor.matmul(CS[0][:], k.ones[:], absw[:, KC, :], start=True, stop=True)
                        for c in range(KC):
                            last = nc.tensor.matmul(CS[1][:], k.ones[:], absw[:, c, :], start=(c == 0), stop=(c == KC - 1))
                        last.then_inc(colsum_done, 1)
                pe.wait_ge(raw_in, 64)
                for j, (parts, r, dst) in enumerate(wt):
                    if j >= 2:
                        pe.wait_ge(wT_sb, j - 1)
                    for q, src in enumerate(parts):
                        last = nc.tensor.transpose(WT[j % 2][:, q * r:(q + 1) * r], src, k.ident[0:r, 0:r])
                    last.then_inc(wT_done, 1)

            @block.scalar
            def _(act):
                def copy_nodes(b):
                    act.wait_ge(gT_done, b + 1)
                    if b >= 2:
                        act.wait_ge(l1_done, (b - 1) * KC)
                    nc.scalar.activation(ctxT[:, b % 2, :], GT[:], ACT.Copy).then_inc(gT_sb, 1)

                def first_layer(b, c):
                    m = b * KC + c
                    act.wait_ge(l1_done, m + 1)
                    if m >= 2:
                        act.wait_ge(h1_ready, m - 1)
                    nc.scalar.activation(ex1[:, c % 2, :], L1[c % 2][:], ACT.Exp, bias=b0t[:, c:c + 1])
                    nc.scalar.activation(re1[:, c % 2, :], L1[c % 2][:], ACT.Relu,
                                         bias=b0t[:, c:c + 1]).then_inc(l1_exp, 1)

                def second_layer(b, t):
                    n = b * TB + t
                    act.wait_ge(s2_ready, n + 1)
                    if n >= 2:
                        act.wait_ge(z2_ready, n - 1)
                    nc.scalar.activation(ex2[:, t % 2, :], s2[:, t % 2, :], ACT.Exp)
                    nc.scalar.activation(re2[:, t % 2, :], s2[:, t % 2, :], ACT.Relu).then_inc(l2_exp, 1)

                act.wait_ge(w_in, 32)
                copy_nodes(0)
                for c in range(KC):
                    first_layer(0, c)
                copy_nodes(1)
                for b in range(B):
                    for t in range(TB):
                        if b + 1 < B:
                            first_layer(b + 1, t)
                        if b + 2 < B and t == TB - 1:
                            copy_nodes(b + 2)
                        second_layer(b, t)
                        if b == 1 and t == 0:
                            nc.scalar.activation(absw[:, KC, :], w0[:], ACT.Abs).then_inc(absw_done, 1)
                            act.wait_ge(w1_in, 16 * (KC + 1))
                        if b == 1:
                            nc.scalar.activation(absw[:, t, :], w1[:, t, :], ACT.Abs).then_inc(absw_done, 1)
                    if b == 1:
                        act.wait_ge(small_in, 80)
                        for j in range(4):
                            nc.scalar.activation(small[:, j, :], small[:, j, :], ACT.Abs,
                                                 accum_out=bounds[:, 3 + j:4 + j]).then_inc(abs_small, 1)
                        nc.scalar.activation(small[:, 4, :], small[:, 4, :], ACT.Abs).then_inc(abs_small, 1)
                    if b == 2:
                        act.wait_ge(gT_done, B)
                        nc.scalar.activation(nodes[:], nodes[:], ACT.Abs).then_inc(abs_small, 1)
                for j, (parts, r, dst) in enumerate(wt):
                    act.wait_ge(wT_done, j + 1)
                    nc.scalar.activation(dst, WT[j % 2][:, 0:r * len(parts)], ACT.Copy).then_inc(wT_sb, 1)

            @block.vector
            def _(dve):
                chain = [0]

                def link(ins):
                    chain[0] += 1
                    ins.then_inc(vch, 1)
                    dve.wait_ge(vch, chain[0])

                def first_layer(b, c):
                    m = b * KC + c
                    dve.wait_ge(l1_exp, m + 1)
                    if b >= 2 and c == 0:
                        dve.wait_ge(l2_done, (b - 1) * TB)
                    nc.vector.scalar_tensor_tensor(h1T[:, b % 2, c, :], ex1[:, c % 2, :], -1.0,
                                                   re1[:, c % 2, :], ALU.add, ALU.min).then_inc(h1_ready, 1)

                def elu2(n):
                    b, t, s = n // TB, n % TB, n % 2
                    dve.wait_ge(l2_exp, n + 1)
                    if b >= 2 and t == 0:
                        dve.wait_ge(feat_out[b % 2], 16)
                    nc.vector.scalar_tensor_tensor(feat[:, b % 2, t, :], ex2[:, s, :], -1.0, re2[:, s, :],
                                                   ALU.add, ALU.min).then_inc(z2_ready, 1)

                ahead = [4, 5, 6, 7, 8, 9, 10, 11, 12, 14, 15] + [NT] * 6

                def largest(n):
                    if n % TB == 0:
                        dve.wait_ge(x_in[n // TB], 16)
                    nc.vector.max(top[:, n, :], k.x[:, n, :]).then_inc(top_ready, 1)
                    nc.vector.bn_stats(bn[:, n, :], k.x[:, n, :]).then_inc(bn_ready, 1)
                    dve.wait_ge(top_ready, n + 1)
                    nc.vector.max_index(top_ix[:, n, :], top[:, n, :], k.x[:, n, :]).then_inc(ix_ready, 1)
                    if n % TB == TB - 1:
                        b = n // TB
                        dve.wait_ge(ix_ready, n + 1)
                        nc.vector.tensor_copy(node[:, b * TB:(b + 1) * TB], top_ix[:, b * TB:(b + 1) * TB, 0]).then_inc(node_ready, 1)

                def add(b):
                    for t in range(TB):
                        n = b * TB + t
                        dve.wait_ge(picked_in[b % 2][t], 16 * (b // 2 + 1))
                        last = nc.vector.tensor_tensor(k.x[:, n, :], k.x[:, n, :], picked[:, b % 2, t, :], ALU.add)
                    link(last)

                def second_layer(b):
                    for t in range(TB):
                        n = b * TB + t
                        if b + 1 < B:
                            first_layer(b + 1, t)
                        dve.wait_ge(l2_done, n + 1)
                        if n >= 2:
                            dve.wait_ge(l2_exp, n - 1)
                        nc.vector.tensor_tensor(s2[:, t % 2, :], L2[t % 2][:], b1bc[:], ALU.add).then_inc(s2_ready, 1)
                        if n:
                            elu2(n - 1)
                        for j in range(ahead[n], ahead[n + 1]):
                            largest(j)
                        if n == NT - 3:
                            moments(0)
                        if n == NT - 2:
                            dve.wait_ge(abs_small, 6)
                            nc.vector.tensor_reduce(rowstat[:, 0:1], nodes[:].rearrange("p t f -> p (t f)"),
                                                    AX_X, ALU.max).then_inc(bounds_ready, 1)

                def moments(b):
                    if b < 2:
                        dve.wait_ge(x2_ready, (b + 1) * TB)
                    for t in range(b * TB, (b + 1) * TB):
                        last = nc.vector.bn_stats(bn2[:, t, :], k.x[:, t, :])
                    link(last)
                    for t in range(b * TB, (b + 1) * TB):
                        last = nc.vector.bn_aggr(k.mv[:, t, :], bn2[:, t, :])
                    link(last)
                    nc.vector.tensor_scalar(k.rstd[:, b * TB:(b + 1) * TB], k.mv[:, b * TB:(b + 1) * TB, 1],
                                            EPS, None, ALU.add).then_inc(var2_ready, 1)

                for c in range(KC):
                    first_layer(0, c)
                for t in range(TB):
                    largest(t)
                for b in range(B - 1):
                    second_layer(b)
                dve.wait_ge(bn_ready, NT)
                for t in range(NT):
                    last = nc.vector.bn_aggr(mv[:, t, :], bn[:, t, :])
                link(last)
                nc.vector.tensor_scalar(rstd[:], mv[:, :, 1], EPS, None, ALU.add).then_inc(var_ready, 1)
                dve.wait_ge(abs_small, 5)
                nc.vector.tensor_tensor(bounds[:, 0:1], bounds[:, 3:4], bounds[:, 4:5], ALU.add)
                nc.vector.tensor_tensor(bounds[:, 1:2], bounds[:, 5:6], bounds[:, 6:7], ALU.add)
                nc.vector.tensor_reduce(bounds[:, 2:3], small[:, 4, :], AX_X, ALU.max).then_inc(bounds_ready, 1)
                dve.wait_ge(colsum_done, 1)
                nc.vector.tensor_reduce(colsum[:, 0:1], CS[0][:], AX_X, ALU.max)
                nc.vector.tensor_reduce(colsum[:, 1:2], CS[1][:], AX_X, ALU.max)
                second_layer(B - 1)
                elu2(NT - 1)
                moments(1)
                add(B - 2)
                moments(2)
                link(nc.vector.tensor_tensor(gap[:], top[:, :, 0], top[:, :, 1], ALU.subtract))
                link(nc.vector.tensor_tensor(lead[:], top[:, :, 0], mv[:, :, 0], ALU.subtract))
                dve.wait_ge(rstd_ready, 1)
                link(nc.vector.tensor_tensor(gap[:], gap[:], rstd[:], ALU.mult))
                link(nc.vector.tensor_tensor(lead[:], lead[:], rstd[:], ALU.mult))
                link(nc.vector.scalar_tensor_tensor(lead[:], lead[:], -1.0, lead[:], ALU.mult, ALU.max))
                link(nc.vector.tensor_scalar(lead[:], lead[:], 1.0, 6e-7, ALU.add, ALU.mult))
                link(nc.vector.scalar_tensor_tensor(gap[:], gap[:], -0.99, lead[:], ALU.mult, ALU.add))
                nc.vector.tensor_reduce(rowstat[:, 1:2], gap[:], AX_X, ALU.max).then_inc(rows_ready, 1)
                dve.wait_ge(reduced, 2)
                f = fin
                link(nc.vector.tensor_tensor(f[:, 0:1], rowstat_max[0:1, 0:1], colsum[0:1, 0:1], ALU.mult))
                link(nc.vector.tensor_tensor(f[:, 1:2], f[:, 0:1], bounds_max[0:1, 2:3], ALU.add))
                link(nc.vector.tensor_tensor(f[:, 1:2], f[:, 1:2], colsum[0:1, 1:2], ALU.mult))
                link(nc.vector.tensor_tensor(f[:, 0:1], f[:, 0:1], bounds_max[0:1, 0:1], ALU.mult))
                link(nc.vector.scalar_tensor_tensor(f[:, 1:2], f[:, 1:2], bounds_max[0:1, 1:2], f[:, 0:1],
                                                    ALU.mult, ALU.add))
                link(nc.vector.tensor_scalar(f[:, 1:2], f[:, 1:2], -2.1 / MASK_VAL, -120.0 / MASK_VAL, ALU.mult, ALU.add))
                add(B - 1)
                dve.wait_ge(reduced, 3)
                link(nc.vector.tensor_tensor(f[:, 2:3], f[:, 1:2], rowstat_max[0:1, 1:2], ALU.add))
                link(nc.vector.tensor_scalar(f[:, 3:4], f[:, 2:3], 0.0, -1.0, ALU.is_lt, ALU.mult))
                link(nc.vector.tensor_scalar(k.flag[:], f[:, 3:4], 1.0, None, ALU.add))


def general_block(nc, k, a):
    with ExitStack() as ctx:
        def sb(name, shape, dt=F32):
            return ctx.enter_context(nc.sbuf_tensor(name, shape, dt))

        loaded = ctx.enter_context(nc.semaphore("g_loaded"))
        nodes_in = ctx.enter_context(nc.semaphore("g_nodes_in"))
        g_passed = ctx.enter_context(nc.semaphore("g_passed"))
        xg = sb("g_x", [P, TB, D])
        cg = sb("g_ctx", [P, TB, FIN])
        bn = sb("g_bn", [P, TB, 6])
        mv = sb("g_mv", [P, TB, 2])
        rstd = sb("g_rstd", [P, TB])
        mhalf = sb("g_mhalf", [P, TB])
        mask = sb("g_mask", [P, TB, N])
        inT = sb("g_inT", [P, KC, N])
        feat = sb("g_feat", [P, TB, H * O])
        work = sb("g_work", [P, TB, N])
        attn = sb("g_attn", [P, 2, TB, H])
        diag = sb("g_diag", [P, TB, P])
        e = sb("g_e", [P, TB, N])
        pT = sb("g_pT", [P, TB, N])
        nmax = sb("g_nmax", [P, TB])
        total = sb("g_total", [P, TB])
        o = sb("g_o", [P, TB, H * O])
        w0 = sb("g_w0", [P, 1, H * O])
        w1 = sb("g_w1", [P, KC, H * O])
        avec = sb("g_avec", [P, 6, H * O])
        bank = k.psum

        def stage(vector=None, scalar=None, tensor=None, gpsimd=None, sync=None):
            with nc.Block() as block:
                if vector:
                    block.vector(lambda dve: vector())
                if scalar:
                    block.scalar(lambda act: scalar())
                if tensor:
                    block.tensor(lambda pe: tensor())
                if gpsimd:
                    block.gpsimd(lambda pool: gpsimd())
                if sync:
                    block.sync(sync)

        def flat(ap):
            return ap.rearrange("p t n -> p (t n)")

        def load_weights(sp):
            sp.dma_start(w0[:, 0, :].rearrange("f (h o) -> f h o", h=H), a["W0"].rearrange("h f o -> f h o")).then_inc(loaded, 16)
            for c in range(KC):
                sp.dma_start(w1[:, c, :].rearrange("f (h o) -> f h o", h=H),
                             a["W1"][:, c * P:(c + 1) * P, :].rearrange("h f o -> f h o")).then_inc(loaded, 16)
            for j, name in enumerate(("a_self0", "a_neigh0", "b0", "a_self1", "a_neigh1", "b1")):
                sp.dma_start(avec[:, j, :], a[name].rearrange("h o -> (h o)").rearrange("(u d) -> u d", u=1)
                             .broadcast_to([P, H * O])).then_inc(loaded, 16)
            sp.wait_ge(loaded, 16 * (1 + KC + 6))
        for engine in (nc.vector, nc.scalar, nc.tensor, nc.gpsimd, nc.sync):
            engine.sem_inc(g_passed, 1)
        stage(sync=load_weights, gpsimd=lambda: nc.gpsimd.memset(mhalf[:], -0.5))

        def each(f, n=TB):
            def run():
                for t in range(n):
                    f(t)
            return run

        def layer(chunks, w, at):
            def products():
                for t in range(TB):
                    for c in range(chunks):
                        nc.tensor.matmul(bank[t][:], inT[:, c, t * P:(t + 1) * P], w[:, c, :],
                                         start=(c == 0), stop=(c == chunks - 1))
            stage(tensor=products)
            stage(scalar=each(lambda t: nc.scalar.activation(feat[:, t, :], bank[t][:], ACT.Copy)))
            for j in range(2):
                stage(vector=each(lambda t: nc.vector.tensor_tensor(work[:, t, :], feat[:, t, :], avec[:, at + j, :], ALU.mult)))
                stage(vector=each(lambda t: nc.vector.tensor_reduce(
                    attn[:, j, t, :], work[:, t, :].rearrange("p (h o) -> p h o", h=H), AX_X, ALU.add)))
            with nc.Fori(0, H) as h:
                stage(vector=each(lambda t: nc.vector.tensor_scalar(
                    diag[:, t, :], k.ident[:], attn[:, 1, t, bass.ds(h, 1)], None, ALU.mult)))
                stage(tensor=each(lambda t: nc.tensor.matmul(bank[5][:, t * P:(t + 1) * P], k.ones[:], diag[:, t, :],
                                                             start=True, stop=True)))
                stage(vector=each(lambda t: nc.vector.tensor_scalar(
                    e[:, t, :], bank[5][:], attn[:, 0, t, bass.ds(h, 1)], None, ALU.add)))
                stage(vector=lambda: nc.vector.scalar_tensor_tensor(flat(work[:]), flat(e[:]), LRELU, flat(e[:]), ALU.mult, ALU.max))
                stage(vector=lambda: nc.vector.tensor_tensor(flat(e[:]), flat(work[:]), flat(mask[:]), ALU.add))
                stage(vector=lambda: nc.vector.tensor_reduce(nmax[:], e[:], AX_X, ALU.max))
                stage(vector=each(lambda t: nc.vector.tensor_scalar(work[:, t, :], e[:, t, :], nmax[:, t:t + 1], None, ALU.subtract)))
                stage(scalar=each(lambda t: nc.scalar.activation(e[:, t, :], work[:, t, :], ACT.Exp, accum_out=total[:, t:t + 1])))
                stage(tensor=each(lambda q: nc.tensor.transpose(bank[q // TB][:, (q % TB) * P:(q % TB + 1) * P],
                                                                e[:, q // TB, (q % TB) * P:(q % TB + 1) * P], k.ident[:]), TB * TB),
                      vector=lambda: nc.vector.reciprocal(nmax[:], total[:]))
                stage(scalar=each(lambda t: nc.scalar.activation(pT[:, t, :], bank[t][:], ACT.Copy)))

                def attend():
                    for t in range(TB):
                        for c in range(TB):
                            nc.tensor.matmul(bank[t][:, 0:O], pT[:, t, c * P:(c + 1) * P], feat[:, c, bass.ds(h * O, O)],
                                             start=(c == 0), stop=(c == TB - 1))
                stage(tensor=attend)
                stage(vector=each(lambda t: nc.vector.tensor_scalar(
                    o[:, t, bass.ds(h * O, O)], bank[t][:, 0:O], nmax[:, t:t + 1], None, ALU.mult)))
            stage(vector=each(lambda t: nc.vector.tensor_tensor(o[:, t, :], o[:, t, :], avec[:, at + 2, :], ALU.add)))
            stage(scalar=lambda: nc.scalar.activation(flat(work[:]), flat(o[:]), ACT.Exp))
            stage(vector=lambda: nc.vector.tensor_scalar(flat(work[:]), flat(work[:]), 1.0, -1.0, ALU.min, ALU.add))
            stage(vector=lambda: nc.vector.tensor_tensor(flat(o[:]), flat(o[:]), flat(work[:]), ALU.max))

        with nc.Fori(0, B) as b:
            def load(sp):
                sp.dma_start(xg[:], a["x"][bass.ds(b, 1)].rearrange("u (t p) d -> p (u t) d", p=P)).then_inc(nodes_in, 16)
                sp.dma_start(cg[:], a["ctx"][bass.ds(b * N, N), :].rearrange("(t p) f -> p t f", p=P)).then_inc(nodes_in, 16)
                sp.wait_ge(nodes_in, (b + 1) * 32)
                sp.sem_inc(g_passed, 1)
            stage(sync=load)
            stage(vector=each(lambda t: nc.vector.bn_stats(bn[:, t, :], xg[:, t, :])),
                  tensor=each(lambda t: nc.tensor.transpose(bank[0][:, t * P:(t + 1) * P], cg[:, t, :], k.ident[:])))
            stage(vector=each(lambda t: nc.vector.bn_aggr(mv[:, t, :], bn[:, t, :])),
                  scalar=lambda: nc.scalar.activation(inT[:, 0, :], bank[0][:], ACT.Copy))
            stage(vector=lambda: nc.vector.tensor_scalar(rstd[:], mv[:, :, 1], EPS, None, ALU.add))
            stage(gpsimd=lambda: nc.gpsimd.tensor_tensor(rstd[:], rstd[:], mhalf[:], ALU.pow))
            stage(vector=each(lambda t: nc.vector.tensor_scalar(work[:, t, :], xg[:, t, :], mv[:, t, 0:1], rstd[:, t:t + 1],
                                                                ALU.subtract, ALU.mult)))
            stage(vector=lambda: nc.vector.tensor_scalar(flat(mask[:]), flat(work[:]), -1.0, 1.0, ALU.mult, ALU.add))
            stage(vector=lambda: nc.vector.tensor_scalar(flat(mask[:]), flat(mask[:]), MASK_VAL, None, ALU.mult))
            layer(1, w0, 0)
            stage(tensor=each(lambda q: nc.tensor.transpose(bank[q // TB][:, (q % TB) * P:(q % TB + 1) * P],
                                                            o[:, q % TB, (q // TB) * P:(q // TB + 1) * P], k.ident[:]), KC * TB))
            stage(scalar=each(lambda c: nc.scalar.activation(inT[:, c, :], bank[c][:], ACT.Copy), KC))
            layer(KC, w1, 3)
            stage(vector=lambda: nc.vector.tensor_tensor(xg[:], xg[:], o[:], ALU.add))
            stage(vector=each(lambda t: nc.vector.bn_stats(bn[:, t, :], xg[:, t, :])))
            stage(vector=each(lambda t: nc.vector.bn_aggr(mv[:, t, :], bn[:, t, :])))
            stage(vector=lambda: nc.vector.tensor_scalar(rstd[:], mv[:, :, 1], EPS, None, ALU.add))
            stage(gpsimd=lambda: nc.gpsimd.tensor_tensor(rstd[:], rstd[:], mhalf[:], ALU.pow))
            stage(vector=lambda: nc.vector.tensor_copy(k.mv[:, bass.ds(b * TB, TB), :], mv[:]))
            stage(vector=lambda: nc.vector.tensor_copy(k.rstd[:, bass.ds(b * TB, TB)], rstd[:]))
            stage(vector=lambda: nc.vector.tensor_copy(k.x[:, bass.ds(b * TB, TB), :], xg[:]))


def experts_block(nc, k, a):
    with ExitStack() as ctx:
        def sb(name, shape, dt=F32):
            return ctx.enter_context(nc.sbuf_tensor(name, shape, dt))

        def sem(name):
            return ctx.enter_context(nc.semaphore(name))

        bank = k.psum
        gateT, upT, downT = k.gateT, k.upT, k.downT
        bn = sb("bn_c", [P, TB, 6])
        lgT = sb("lgT", [E, N])
        rows = sb("rows", [P, 2, TB, ROW])
        xnT = sb("xnT", [P, KC, T])
        top = sb("top_c", [P, TB, 8])
        nmax = sb("nmax", [P, TB])
        lg = sb("lg", [P, TB, E])
        ex = sb("ex", [P, TB, E])
        esum = sb("esum", [P, TB])
        rsum = sb("rsum", [P, TB])
        key = sb("key", [P, TB, E])
        ktop = sb("ktop", [P, TB, 8])
        kix = sb("kix", [P, TB, 8], U32)
        kixf = sb("kixf", [P, TB, 8])
        krep = sb("krep", [P, TB, E])
        iota_e, order = k.iota_e, k.order
        left = sb("left", [P, NT * E])
        val = sb("val", [P, HALF])
        cand = sb("cand", [P, CAP])
        both = sb("both", [E, 2 * CAP])
        slots = sb("slots", [E, CAP])
        late = sb("late", [E, CAP])
        table = sb("table", [P, E], U32)
        sg = sb("sg", [P, 2, N])
        shid = sb("shid", [P, 2, SC, N])
        gu_w = sb("gu_w", [P, U, KC, 2 * I])
        dn_w = sb("dn_w", [IH, U, 2, D])
        gx = sb("gx", [P, U, ROW])
        gxT = sb("gxT", [P, 2, KC, P])
        slot_w = sb("slot_w", [P, 2, 1])
        eg = sb("eg", [P, I])
        hid = sb("hid", [P, 2, IH])
        hidT = sb("hidT", [IH, 2, 2, P])
        y = sb("y", [P, 2, D])
        idx_g = sb("idx_g", [P, U, 1], U32)
        idx_s = sb("idx_s", [P, 2, 1], U32)

        lg_ready, lgT_done, lgT_sb = sem("lg_ready"), sem("lgT_done"), sem("lgT_sb")
        rows_out = [sem(f"rows_out{j}") for j in range(2)]
        vch = sem("vch_c")
        pool_passed = sem("pool_passed")
        var_ready, rstd_ready, xn_ready, xT_done, xT_sb = (
            sem(s) for s in ("var_ready_c", "rstd_ready_c", "xn_ready", "xT_done", "xT_sb"))
        logits, nmax_ready, exp_done, rows_full, left_ready, leftT_done, val_ready = (
            sem(s) for s in ("logits", "nmax_ready", "exp_done", "rows_full", "left_ready", "leftT_done", "val_ready"))
        cand_ready, both_in, slots_ready, slotsT_done, table_ready = (
            sem(s) for s in ("cand_ready", "both_in", "slots_ready", "slotsT_done", "table_ready"))
        sup_done, sg_ready, shid_ready, sdn_done, x3_ready, x3_out = (
            sem(s) for s in ("sup_done", "sg_ready", "shid_ready", "sdn_done", "x3_ready", "x3_out"))
        w_in = [sem(f"ew_in{u}") for u in range(U)]
        g_in = [sem(f"eg_in{u}") for u in range(U)]
        pidx, gT_done, gxT_ready, w_copied, gu_done, eg_ready, hid_ready, hT_done, hidT_ready, dn_done, y_ready, y_free, scat = (
            sem(s) for s in ("pidx", "egT_done", "gxT_ready", "w_copied", "gu_done", "eg_ready", "hid_ready",
                             "hT_done", "hidT_ready", "dn_done", "y_ready", "y_free", "scat"))

        XT, LG, UP, SD = bank[0:2], bank[2], bank[3:7], bank[0:2]
        LEFT, LT = (bank[2], bank[7]), bank[7]
        GT, GU, HT, DN = (bank[2], bank[7]), bank[3:5], bank[5], bank[6]

        with nc.Block() as block:
            def load_expert(sp, e, u):
                def of(name):
                    w = a[name]
                    return w[e] if isinstance(e, int) else w[bass.ds(e, 1)].rearrange("u r n -> (u r) n")
                sp.dma_start(gu_w[:, u, :, :], of("gate_up").rearrange("(p c) n -> p c n", c=KC)).then_inc(w_in[u], 16)
                sp.dma_start(dn_w[:, u, :, :], of("down").rearrange("(p j) n -> p j n", j=2)).then_inc(w_in[u], 16)

            @block.sync
            def _(sp):
                for u in range(U):
                    load_expert(sp, u, u)
                for b in range(B):
                    sp.wait_ge(rows_full, b + 1)
                    sp.dma_start(a["rows_dram"][b * N:(b + 1) * N, :].rearrange("(t p) r -> p t r", p=P),
                                 rows[:, b % 2]).then_inc(rows_out[b % 2], 16)
                sp.wait_ge(cand_ready, 1)
                sp.dma_start(both[:, 0:CAP], cand[0:E, :]).then_inc(both_in, 16)
                sp.dma_start(both[:, CAP:2 * CAP], cand[E:2 * E, :]).then_inc(both_in, 16)
                for b in range(B):
                    sp.wait_ge(x3_ready, (b + 1) * TB)
                    sp.dma_start(a["out"][b * N:(b + 1) * N, :].rearrange("(t p) d -> p t d", p=P),
                                 k.x[:, b * TB:(b + 1) * TB, :]).then_inc(x3_out, 16)
                with sp.Fori(1, E // U) as i:
                    for u in range(U):
                        sp.wait_ge(dn_done, (i - 1) * U + u + 1)
                        load_expert(sp, i * U + u, u)

            @block.gpsimd
            def _(pool):
                pool.wait_ge(var_ready, 1)
                nc.gpsimd.tensor_tensor(k.rstd[:, (B - 1) * TB:NT], k.rstd[:, (B - 1) * TB:NT], k.mhalf[:, 0:TB], ALU.pow).then_inc(rstd_ready, 1)

                def scatter(e, u):
                    if not (isinstance(e, int) and e == 0):
                        if due(e * 16):
                            pool.wait_ge(scat, e * 16)
                        pool.sem_inc(pool_passed, 1)
                    nc.gpsimd.tensor_copy(idx_s[:, u % 2, :], table[:, bass.ds(e, 1)]).then_inc(y_free, 1)
                    pool.wait_ge(y_free, e + 1)
                    pool.wait_ge(y_ready, e + 1)
                    pool.sem_inc(pool_passed, 1)
                    pool.indirect_dma_start(a["out"][:, :], bass.IndirectOffsetOnAxis(ap=idx_s[:, u % 2, :], axis=0),
                                            y[:, u % 2, :], None, compute_op=ALU.add).then_inc(scat, 16)

                pool.wait_ge(table_ready, 1)
                for j in range(2):
                    pool.wait_ge(rows_out[j], 16 * B // 2)
                for e in range(U - 1):
                    nc.gpsimd.tensor_copy(idx_g[:, e, :], table[:, e:e + 1]).then_inc(pidx, 1)
                    pool.wait_ge(pidx, e + 1)
                    pool.indirect_dma_start(gx[:, e, :], None, a["rows_dram"][:, :],
                                            bass.IndirectOffsetOnAxis(ap=idx_g[:, e, :], axis=0)).then_inc(g_in[e], 16)

                def gather_ahead(n, i, u):
                    e, s = n + U - 1, (u + U - 1) % U
                    if not (isinstance(n, int) and n == 0):
                        if due(n):
                            pool.wait_ge(gT_done, n)
                        if due(n):
                            pool.wait_ge(w_copied, n)
                        pool.sem_inc(pool_passed, 1)
                    nc.gpsimd.tensor_copy(idx_g[:, s, :], table[:, bass.ds(e, 1)]).then_inc(pidx, 1)
                    pool.wait_ge(pidx, n + U)
                    pool.sem_inc(pool_passed, 1)
                    pool.indirect_dma_start(gx[:, s, :], None, a["rows_dram"][:, :],
                                            bass.IndirectOffsetOnAxis(ap=idx_g[:, s, :], axis=0)).then_inc(g_in[s], 16)

                def turn(i, last):
                    for u in range(U):
                        n = i * U + u
                        if not (last and u > 0):
                            gather_ahead(n, i, u)
                        scatter(n, u)
                pool.wait_ge(x3_out, 16 * B)
                for i in turns(pool, E // U - 1):
                    turn(i, False)
                turn(E // U - 1, True)
                pool.wait_ge(scat, 16 * E)

            @block.tensor
            def _(pe):
                def gate(b):
                    for t in range(TB):
                        n = b * TB + t
                        pe.wait_ge(xn_ready, n + 1)
                        if n >= 2:
                            pe.wait_ge(xT_sb, n - 1)
                        for c in range(KC):
                            last = nc.tensor.transpose(XT[t % 2][:, c * P:(c + 1) * P], rows[:, b % 2, t, c * P:(c + 1) * P],
                                                       k.ident[:])
                        last.then_inc(xT_done, 1)
                    if b:
                        pe.wait_ge(lgT_sb, b)
                    pe.wait_ge(xT_sb, (b + 1) * TB)
                    for c in range(KC):
                        last = nc.tensor.matmul(LG[0:E, :], gateT[:, c, :], xnT[:, c, b * N:(b + 1) * N],
                                                start=(c == 0), stop=(c == KC - 1))
                    last.then_inc(lgT_done, 1)

                def logits_back(b):
                    pe.wait_ge(lgT_sb, b + 1)
                    if b:
                        pe.wait_ge(lg_ready, b)
                    for t in range(TB):
                        last = nc.tensor.transpose(LT[:, t * E:(t + 1) * E], lgT[:, t * P:(t + 1) * P], k.ident[0:E, 0:E])
                    last.then_inc(logits, 1)

                def shared_up(b, s):
                    m = b * SC + s
                    if m >= 2:
                        pe.wait_ge(sg_ready, m - 1)
                        pe.wait_ge(shid_ready, m - 1)
                    for g in range(2):
                        for c in range(KC):
                            last = nc.tensor.matmul(UP[2 * (m % 2) + g][:], upT[:, c, g * SI + s * P:g * SI + (s + 1) * P],
                                                    xnT[:, c, b * N:(b + 1) * N], start=(c == 0), stop=(c == KC - 1))
                        last.then_inc(sup_done, 1)

                def shared_down(b):
                    for t in range(TB):
                        n = b * TB + t
                        if n >= 2:
                            pe.wait_ge(x3_ready, n - 1)
                        for s in range(SC):
                            if t == 0:
                                pe.wait_ge(shid_ready, b * SC + s + 1)
                            last = nc.tensor.matmul(SD[t % 2][:], shid[:, b % 2, s, t * P:(t + 1) * P], downT[:, s, :],
                                                    start=(s == 0), stop=(s == SC - 1))
                        last.then_inc(sdn_done, 1)

                gate(0)
                logits_back(0)
                gate(1)
                shared_up(0, 0)
                logits_back(1)
                shared_up(0, 1)
                gate(2)
                shared_up(0, 2)
                logits_back(2)
                gate(3)
                shared_up(1, 0)
                logits_back(3)
                shared_up(1, 1)
                pe.wait_ge(left_ready, B)
                for j in range(NT // 2):
                    last = nc.tensor.transpose(LEFT[j // 4][:, (j % 4) * P:(j % 4 + 1) * P],
                                               left[:, j * 2 * E:(j + 1) * 2 * E], k.ident[:])
                    if j % 4 == 3:
                        last.then_inc(leftT_done, 1)
                pe.wait_ge(xT_sb, NT)
                shared_down(0)
                shared_up(1, 2)
                shared_down(1)
                for s in range(SC):
                    shared_up(2, s)
                shared_up(3, 0)
                shared_down(2)
                shared_up(3, 1)
                shared_up(3, 2)
                pe.wait_ge(slots_ready, 1)
                nc.tensor.transpose(bank[7][:, 0:E], slots[:], k.ident[0:E, 0:E]).then_inc(slotsT_done, 1)
                shared_down(3)

                def transposes(n, u, i1):
                    pe.wait_ge(g_in[u % U], 16 * i1)
                    for c in range(KC):
                        last = nc.tensor.transpose(GT[u % 2][:, c * P:(c + 1) * P], gx[:, u % U, c * P:(c + 1) * P], k.ident[:])
                    last.then_inc(gT_done, 1)

                def down(n, u):
                    pe.wait_ge(hidT_ready, n + 1)
                    if due(n):
                        pe.wait_ge(y_ready, n)
                    for j in range(2):
                        last = nc.tensor.matmul(DN[:], hidT[:, u % 2, j, :], dn_w[:, u % U, j, :],
                                                start=(j == 0), stop=(j == 1))
                    last.then_inc(dn_done, 1)

                def step(i, u, first, last_step):
                    n = i * U + u
                    pe.wait_ge(w_in[u], (i + 1) * 32)
                    pe.wait_ge(gxT_ready, n + 1)
                    for c in range(KC):
                        last = nc.tensor.matmul(GU[u % 2][:, 0:2 * I], gxT[:, u % 2, c, :], gu_w[:, u, c, :],
                                                start=(c == 0), stop=(c == KC - 1))
                    last.then_inc(gu_done, 1)
                    if not last_step:
                        transposes(n + 1, u + 1, i + 1 + (u + 1) // U)
                    if not first:
                        down(n - 1, (u - 1) % U)
                    pe.wait_ge(hid_ready, n + 1)
                    for j in range(2):
                        last = nc.tensor.transpose(HT[0:IH, j * P:(j + 1) * P], hid[:, j, :], k.ident[:])
                    last.then_inc(hT_done, 1)

                pe.wait_ge(table_ready, 1)
                transposes(0, 0, 1)
                for u in range(U):
                    step(0, u, u == 0, False)
                with pe.Fori(1, E // U - 1) as i:
                    for u in range(U):
                        step(i, u, False, False)
                for u in range(U):
                    step(E // U - 1, u, False, u == U - 1)
                down(E - 1, U - 1)

            @block.scalar
            def _(act):
                def transposed(b):
                    for t in range(TB):
                        n = b * TB + t
                        act.wait_ge(xT_done, n + 1)
                        nc.scalar.activation(xnT[:, :, n * P:(n + 1) * P], XT[t % 2][:].rearrange("p (c q) -> p c q", c=KC),
                                             ACT.Copy).then_inc(xT_sb, 1)

                def logits_copy(b):
                    act.wait_ge(lgT_done, b + 1)
                    if b:
                        act.wait_ge(logits, b)
                    nc.scalar.activation(lgT[:], LG[0:E, :], ACT.Copy).then_inc(lgT_sb, 1)

                def gate_exp(b):
                    act.wait_ge(nmax_ready, b + 1)
                    if b:
                        act.wait_ge(rows_full, b)
                    for t in range(TB):
                        last = nc.scalar.activation(ex[:, t, :], lg[:, t, :], ACT.Exp, bias=nmax[:, t:t + 1],
                                                    accum_out=esum[:, t:t + 1])
                    last.then_inc(exp_done, 1)

                def silu(b, s):
                    m = b * SC + s
                    act.wait_ge(sup_done, 2 * m + 1)
                    if m >= 2:
                        act.wait_ge(shid_ready, m - 1)
                    nc.scalar.activation(sg[:, m % 2, :], UP[2 * (m % 2)][:], ACT.Silu).then_inc(sg_ready, 1)

                transposed(0)
                logits_copy(0)
                transposed(1)
                logits_copy(1)
                gate_exp(0)
                silu(0, 0)
                silu(0, 1)
                gate_exp(1)
                transposed(2)
                logits_copy(2)
                silu(0, 2)
                transposed(3)
                gate_exp(2)
                logits_copy(3)
                silu(1, 0)
                gate_exp(3)
                silu(1, 1)
                silu(1, 2)
                for b in (2, 3):
                    for s in range(SC):
                        silu(b, s)

                def gx_copy(n, u):
                    act.wait_ge(gT_done, n + 1)
                    nc.scalar.activation(gxT[:, u % 2, :, :].rearrange("p c q -> p (c q)"), GT[u % 2][:],
                                         ACT.Copy).then_inc(gxT_ready, 1)

                def step(i, u, last_step):
                    n = i * U + u
                    act.wait_ge(gu_done, n + 1)
                    if due(n):
                        act.wait_ge(hid_ready, n)
                    nc.scalar.activation(eg[:], GU[u % 2][:, 0:I], ACT.Silu).then_inc(eg_ready, 1)
                    if not last_step:
                        gx_copy(n + 1, u + 1)
                gx_copy(0, 0)
                for i in turns(act, E // U - 1):
                    for u in range(U):
                        step(i, u, False)
                for u in range(U):
                    step(E // U - 1, u, u == U - 1)

            @block.vector
            def _(dve):
                chain = [0]

                def link(ins):
                    chain[0] += 1
                    ins.then_inc(vch, 1)
                    dve.wait_ge(vch, chain[0])

                def last_moments():
                    for t in range(TB):
                        last = nc.vector.bn_stats(bn[:, t, :], k.x[:, (B - 1) * TB + t, :])
                    link(last)
                    for t in range(TB):
                        last = nc.vector.bn_aggr(k.mv[:, (B - 1) * TB + t, :], bn[:, t, :])
                    link(last)
                    nc.vector.tensor_scalar(k.rstd[:, (B - 1) * TB:NT], k.mv[:, (B - 1) * TB:NT, 1], EPS, None, ALU.add).then_inc(var_ready, 1)

                def norm(b):
                    if b == B - 1:
                        dve.wait_ge(rstd_ready, 1)
                    if b >= 2:
                        dve.wait_ge(rows_out[b % 2], 16)
                        dve.wait_ge(xT_done, (b - 1) * TB)
                    for t in range(TB):
                        nc.vector.tensor_scalar(
                            rows[:, b % 2, t, 0:D].rearrange("q (c p) -> q c p", c=KC),
                            k.x[:, b * TB + t, :].rearrange("q (p c) -> q c p", c=KC),
                            k.mv[:, b * TB + t, 0:1], k.rstd[:, b * TB + t:b * TB + t + 1], ALU.subtract, ALU.mult).then_inc(xn_ready, 1)

                def route(b):
                    dve.wait_ge(logits, b + 1)
                    if b:
                        dve.wait_ge(exp_done, b)
                    nc.vector.tensor_copy(lg[:].rearrange("p t e -> p (t e)"), LT[:, 0:TB * E]).then_inc(lg_ready, 1)
                    dve.wait_ge(lg_ready, b + 1)
                    for t in range(TB):
                        last = nc.vector.max(top[:, t, :], lg[:, t, :])
                    link(last)
                    nc.vector.tensor_scalar(nmax[:], top[:, :, 0], -1.0, None, ALU.mult).then_inc(nmax_ready, 1)
                    for t in range(TB):
                        last = nc.vector.tensor_scalar(key[:, t, :], lg[:, t, :], top[:, t, 0:1], EXP_FLOOR,
                                                       ALU.subtract, ALU.max)
                    link(last)
                    for t in range(TB):
                        last = nc.vector.max(ktop[:, t, :], key[:, t, :])
                    link(last)
                    for t in range(TB):
                        nc.vector.match_replace(krep[:, t, :], ktop[:, t, :], key[:, t, :], -1000.0)
                        last = nc.vector.max_index(kix[:, t, :], ktop[:, t, :], key[:, t, :])
                    link(last)
                    nc.vector.tensor_copy(kixf[:], kix[:])
                    link(nc.vector.tensor_scalar(krep[:], krep[:], -500.0, None, ALU.is_gt))
                    for j in (TOPK, TOPK + 1):
                        for t in range(TB):
                            last = nc.vector.scalar_tensor_tensor(krep[:, t, :], iota_e[:], kixf[:, t, j:j + 1],
                                                                  krep[:, t, :], ALU.is_equal, ALU.add)
                        link(last)
                    nc.vector.tensor_copy(left[:, b * TB * E:(b + 1) * TB * E],
                                          krep[:].rearrange("p t e -> p (t e)")).then_inc(left_ready, 1)
                    dve.wait_ge(exp_done, b + 1)
                    nc.vector.reciprocal(rsum[:], esum[:])
                    link(nc.vector.scalar_tensor_tensor(ex[:], krep[:], 0.0, ex[:], ALU.is_equal, ALU.mult))
                    for t in range(TB):
                        last = nc.vector.tensor_scalar(rows[:, b % 2, t, D:ROW], ex[:, t, :], rsum[:, t:t + 1], None, ALU.mult)
                    last.then_inc(rows_full, 1)
                    dve.wait_ge(rows_full, b + 1)

                def shared_up(b, s):
                    m = b * SC + s
                    dve.wait_ge(sup_done, 2 * m + 2)
                    dve.wait_ge(sg_ready, m + 1)
                    if s == 0 and b >= 2:
                        dve.wait_ge(sdn_done, (b - 1) * TB)
                    nc.vector.tensor_tensor(shid[:, b % 2, s, :], UP[2 * (m % 2) + 1][:], sg[:, m % 2, :], ALU.mult).then_inc(shid_ready, 1)

                def shared_down(b, t):
                    n = b * TB + t
                    dve.wait_ge(sdn_done, n + 1)
                    nc.vector.tensor_tensor(k.x[:, n, :], SD[t % 2][:], k.x[:, n, :], ALU.add).then_inc(x3_ready, 1)

                def extract(r):
                    link(nc.vector.max(cand[:, r * 8:(r + 1) * 8], val[:]))
                    last = nc.vector.match_replace(val[:], cand[:, r * 8:(r + 1) * 8], val[:], 0.0)
                    if r == R - 1:
                        last.then_inc(cand_ready, 1)
                    else:
                        link(last)

                def merge(r):
                    link(nc.vector.max(slots[:, r * 8:(r + 1) * 8], both[:]))
                    if r < R - 1:
                        link(nc.vector.match_replace(both[:], slots[:, r * 8:(r + 1) * 8], both[:], 0.0))

                R = CAP // 8
                norm(0)
                norm(1)
                last_moments()
                route(0)
                shared_up(0, 0)
                norm(2)
                route(1)
                shared_up(0, 1)
                norm(3)
                shared_up(0, 2)
                route(2)
                shared_up(1, 0)
                route(3)
                shared_up(1, 1)
                for q in range(2):
                    dve.wait_ge(leftT_done, q + 1)
                    link(nc.vector.scalar_tensor_tensor(val[:, q * 512:(q + 1) * 512], LEFT[q][:], -2.0 * T,
                                                        order[:, q * 512:(q + 1) * 512], ALU.mult, ALU.add))
                rounds = iter(range(R))
                for t in range(TB):
                    shared_down(0, t)
                    if t < 3:
                        extract(next(rounds))
                shared_up(1, 2)
                for t in range(TB):
                    extract(next(rounds))
                    shared_down(1, t)
                for s in range(2):
                    for _ in range(3):
                        extract(next(rounds))
                    shared_up(2, s)
                for r in rounds:
                    extract(r)
                shared_up(2, 2)
                dve.wait_ge(both_in, 32)
                shared_up(3, 0)
                for t in range(TB):
                    for r in (2 * t, 2 * t + 1):
                        merge(r)
                    shared_down(2, t)
                for r in range(2 * TB, R):
                    merge(r)
                link(nc.vector.tensor_scalar(late[:], slots[:], float(T) + 0.5, 2.0 * T, ALU.is_gt, ALU.mult))
                link(nc.vector.scalar_tensor_tensor(late[:], late[:], float(T), slots[:], ALU.add, ALU.subtract))
                nc.vector.tensor_copy(slots[:], late[:]).then_inc(slots_ready, 1)
                shared_up(3, 1)
                shared_up(3, 2)
                dve.wait_ge(slotsT_done, 1)
                nc.vector.tensor_copy(table[:], bank[7][:, 0:E]).then_inc(table_ready, 1)
                for t in range(TB):
                    shared_down(3, t)

                def scaled(n, u):
                    dve.wait_ge(dn_done, n + 1)
                    dve.wait_ge(y_free, n + 1)
                    nc.vector.tensor_scalar(y[:, u % 2, :], DN[:], slot_w[:, u % 2, :], None, ALU.mult).then_inc(y_ready, 1)

                def step(i, u, first):
                    n = i * U + u
                    dve.wait_ge(gT_done, n + 1)
                    if not (isinstance(n, int) and n < 2):
                        if due(n - 1):
                            dve.wait_ge(y_ready, n - 1)
                    nc.vector.tensor_copy(slot_w[:, u % 2, :], gx[:, u, bass.ds(n + D, 1)]).then_inc(w_copied, 1)
                    dve.wait_ge(eg_ready, n + 1)
                    if due(n):
                        dve.wait_ge(hT_done, n)
                    nc.vector.tensor_tensor(hid[:].rearrange("s j p -> s p j"), GU[u % 2][:, I:2 * I].rearrange("s (p j) -> s p j", j=2),
                                            eg[:].rearrange("s (p j) -> s p j", j=2), ALU.mult).then_inc(hid_ready, 1)
                    if not first:
                        scaled(n - 1, (u - 1) % U)
                    dve.wait_ge(hT_done, n + 1)
                    nc.vector.tensor_copy(hidT[:, u % 2, :, :].rearrange("p j q -> p (j q)"), HT[0:IH, 0:2 * P]).then_inc(hidT_ready, 1)
                for u in range(U):
                    step(0, u, u == 0)
                with dve.Fori(1, E // U) as i:
                    for u in range(U):
                        step(i, u, False)
                scaled(E - 1, U - 1)


def build(nc, a):
    k = Kernel()
    with ExitStack() as ctx:
        allocate(nc, ctx, k)
        attention_block(nc, k, a)
        flag = nc.values_load(k.flag[0:1, 0:1], min_val=0, max_val=1)
        with nc.If(flag > 0):
            general_block(nc, k, a)
        nc.end_ifs()
        experts_block(nc, k, a)


_INS = {"x": "x", "ctx_512": "ctx", "L0_xattn_W0": "W0", "L0_xattn_a_self0": "a_self0",
        "L0_xattn_a_neigh0": "a_neigh0", "L0_xattn_b0": "b0", "L0_xattn_W1": "W1",
        "L0_xattn_a_self1": "a_self1", "L0_xattn_a_neigh1": "a_neigh1", "L0_xattn_b1": "b1",
        "L0_ffn_gate_w": "gate_w", "L0_ffn_gate_up_proj": "gate_up", "L0_ffn_down_proj": "down",
        "L0_ffn_shared_gate_w": "sh_gate", "L0_ffn_shared_up_w": "sh_up", "L0_ffn_shared_down_w": "sh_down"}


def kernel(**inputs):
    import numpy as _np
    import concourse.bacc as _bacc
    from concourse.bass_utils import run_bass_kernel_spmd as _run

    nc = _bacc.Bacc("TRN2", target_bir_lowering=False, num_devices=1)
    arrays, a = {}, {}
    for name, short in _INS.items():
        v = _np.ascontiguousarray(inputs[name])
        if short == "ctx":
            v = v.reshape(T, FIN)
        arrays[f"in_{short}"] = v
        a[short] = nc.dram_tensor(f"in_{short}", v.shape, mybir.dt.from_np(v.dtype), kind="ExternalInput").ap()
    a["out"] = nc.dram_tensor("out", (T, D), F32, kind="ExternalOutput").ap()
    for b in range(B):
        a[f"node_dram{b}"] = nc.dram_tensor(f"node_dram{b}", (N, 1), U32, kind="Internal").ap()
        a[f"feat_dram{b}"] = nc.dram_tensor(f"feat_dram{b}", (N, D), F32, kind="Internal").ap()
    a["rows_dram"] = nc.dram_tensor("rows_dram", (T, ROW), F32, kind="Internal").ap()
    build(nc, a)
    r = _run(nc, [arrays], core_ids=[0])
    return r.results[0]["out"].reshape(B, N, D)
```
